# Optimizing a Trainium2 kernel written in Bass

```python
import numpy as np
import jax
import jax.numpy as jnp

def _softmax(x, axis=-1):
    return jax.nn.softmax(x, axis=axis)

def _gelu(x):
    return jax.nn.gelu(x, approximate=True)

def _silu(x):
    return jax.nn.silu(x)

def _sigmoid(x):
    return jax.nn.sigmoid(x)

def _layernorm(x, axis=-1, eps=1e-05):
    m = jnp.mean(x, axis=axis, keepdims=True)
    v = jnp.var(x, axis=axis, keepdims=True)
    return (x - m) / jnp.sqrt(v + eps)

def _scatter_add(tgt, idx, src, axis=0):
    return tgt.at[idx].add(src)

def _segment_sum(src, seg, n):
    return jax.ops.segment_sum(src, seg, n)
kernel_name = 'mk_lm_tower_d1_tok_ids1024_r4_20980b'

def setup_inputs(seed: int=0):
    np.random.seed(seed)
    _w = jnp.asarray

    def _rec_inputs():
        import jax
        import jax.numpy as jnp
        _rk = jax.random.key(seed)
        x = jax.random.randint(jax.random.fold_in(_rk, 1), (8, 2048), 0, 12564, jnp.int32)
        return x
    x = _rec_inputs()

    def _L0_tok_setup():
        import jax, jax.numpy as jnp
        import numpy as np
        VOCAB = 50257
        NUM_DIM = 256
        BATCH = 4
        SEQ = 1024
        key = jax.random.key(seed)
        k_tok, k_w, k_b = jax.random.split(key, 3)
        tokens = jax.random.randint(k_tok, (BATCH, SEQ), 0, VOCAB)
        weight = jax.random.normal(k_w, (NUM_DIM, VOCAB), dtype=jnp.float32) * 0.02
        bias = jax.random.normal(k_b, (NUM_DIM,), dtype=jnp.float32) * 0.02
        return {'tokens': tokens, 'weight': weight, 'bias': bias}
    _L0_tok_all = _L0_tok_setup()
    _L0_tok_in = {k: v for k, v in _L0_tok_all.items() if k in ('weight', 'bias')}
    del _L0_tok_all

    def _L0_attn_setup():
        import jax, jax.numpy as jnp
        import numpy as np
        D = 256
        N = 64
        EPS = 1e-06
        key = jax.random.key(seed)
        ks = jax.random.split(key, 10)
        sD = 1.0 / np.sqrt(D)
        sN = 1.0 / np.sqrt(N)
        x = jax.random.normal(ks[0], (8, 1024, D), dtype=jnp.float32)
        A_log = jax.random.normal(ks[1], (N,), dtype=jnp.float32)
        WB = jax.random.uniform(ks[2], (N, D), jnp.float32, -sD, sD)
        bB = jax.random.uniform(ks[3], (N,), jnp.float32, -sD, sD)
        WC = jax.random.uniform(ks[4], (N, D), jnp.float32, -sD, sD)
        bC = jax.random.uniform(ks[5], (N,), jnp.float32, -sD, sD)
        Wd = jax.random.uniform(ks[6], (1, D), jnp.float32, -sD, sD)
        bd = jax.random.uniform(ks[7], (1,), jnp.float32, -sD, sD)
        Wo = jax.random.uniform(ks[8], (D, N), jnp.float32, -sN, sN)
        bo = jax.random.uniform(ks[9], (D,), jnp.float32, -sN, sN)
        return {'x': x, 'A_log': A_log, 'WB': WB, 'bB': bB, 'WC': WC, 'bC': bC, 'Wd': Wd, 'bd': bd, 'Wo': Wo, 'bo': bo}
    _L0_attn_all = _L0_attn_setup()
    _L0_attn_in = {k: v for k, v in _L0_attn_all.items() if k in ('A_log', 'WB', 'bB', 'WC', 'bC', 'Wd', 'bd', 'Wo', 'bo')}
    del _L0_attn_all

    def _L0_ffn_setup():
        import jax, jax.numpy as jnp
        import numpy as np
        LN_EPS = 1e-05

        def layer_norm(x, g, b):
            mu = jnp.mean(x, axis=-1, keepdims=True)
            var = jnp.mean(jnp.square(x - mu), axis=-1, keepdims=True)
            return (x - mu) * jax.lax.rsqrt(var + LN_EPS) * g + b

        def ternary_quant(w):
            scale = 1.0 / jnp.clip(jnp.mean(jnp.abs(w)), 1e-05)
            wq = jnp.clip(jnp.round(w * scale), -1.0, 1.0) / scale
            return w + jax.lax.stop_gradient(wq - w)
        key = jax.random.key(seed)
        ks = jax.random.split(key, 3)
        dim, hidden = (256, 1024)
        B, S = (8, 256)
        x = jax.random.normal(ks[0], (B, S, dim), dtype=jnp.float32)
        w1 = jax.random.normal(ks[1], (hidden, dim), dtype=jnp.float32) * 0.02
        w2 = jax.random.normal(ks[2], (dim, hidden), dtype=jnp.float32) * 0.02
        return {'x': x, 'ln1_g': jnp.ones((dim,), jnp.float32), 'ln1_b': jnp.zeros((dim,), jnp.float32), 'w1': w1, 'b1': jnp.zeros((hidden,), jnp.float32), 'ln2_g': jnp.ones((hidden,), jnp.float32), 'ln2_b': jnp.zeros((hidden,), jnp.float32), 'w2': w2, 'b2': jnp.zeros((dim,), jnp.float32)}
    _L0_ffn_all = _L0_ffn_setup()
    _L0_ffn_in = {k: v for k, v in _L0_ffn_all.items() if k in ('ln1_g', 'ln1_b', 'w1', 'b1', 'ln2_g', 'ln2_b', 'w2', 'b2')}
    del _L0_ffn_all
    return {'x': x, 'L0_tok_weight': _L0_tok_in['weight'], 'L0_tok_bias': _L0_tok_in['bias'], 'L0_attn_A_log': _L0_attn_in['A_log'], 'L0_attn_WB': _L0_attn_in['WB'], 'L0_attn_bB': _L0_attn_in['bB'], 'L0_attn_WC': _L0_attn_in['WC'], 'L0_attn_bC': _L0_attn_in['bC'], 'L0_attn_Wd': _L0_attn_in['Wd'], 'L0_attn_bd': _L0_attn_in['bd'], 'L0_attn_Wo': _L0_attn_in['Wo'], 'L0_attn_bo': _L0_attn_in['bo'], 'L0_ffn_ln1_g': _L0_ffn_in['ln1_g'], 'L0_ffn_ln1_b': _L0_ffn_in['ln1_b'], 'L0_ffn_w1': _L0_ffn_in['w1'], 'L0_ffn_b1': _L0_ffn_in['b1'], 'L0_ffn_ln2_g': _L0_ffn_in['ln2_g'], 'L0_ffn_ln2_b': _L0_ffn_in['ln2_b'], 'L0_ffn_w2': _L0_ffn_in['w2'], 'L0_ffn_b2': _L0_ffn_in['b2']}

def reference(x, L0_tok_weight, L0_tok_bias, L0_attn_A_log, L0_attn_WB, L0_attn_bB, L0_attn_WC, L0_attn_bC, L0_attn_Wd, L0_attn_bd, L0_attn_Wo, L0_attn_bo, L0_ffn_ln1_g, L0_ffn_ln1_b, L0_ffn_w1, L0_ffn_b1, L0_ffn_ln2_g, L0_ffn_ln2_b, L0_ffn_w2, L0_ffn_b2):
    import jax
    import jax.numpy as jnp

    def _L0_tok_ref(tokens, weight, bias):
        import jax, jax.numpy as jnp
        import numpy as np
        VOCAB = 50257
        NUM_DIM = 256
        BATCH = 4
        SEQ = 1024
        table = weight.T
        return jnp.take(table, tokens, axis=0) + bias

    def _L0_attn_ref(x, A_log, WB, bB, WC, bC, Wd, bd, Wo, bo):
        import jax, jax.numpy as jnp
        import numpy as np
        D = 256
        N = 64
        EPS = 1e-06
        A = -jax.nn.softplus(A_log)
        B_t = jnp.einsum('bld,nd->bln', x, WB) + bB
        _C_proj = jnp.einsum('bld,nd->bln', x, WC) + bC
        Delta = jax.nn.softplus(jnp.einsum('bld,nd->bln', x, Wd) + bd)
        dA = jnp.exp(A * Delta)
        dB = (dA - 1.0) / (A + EPS) * B_t
        conv = jnp.cumprod(dA, axis=1)
        ones = jnp.ones_like(dA[:, :1, :])
        Ct = jnp.concatenate([ones, conv[:, :-1, :]], axis=1)
        z = dB / (Ct + EPS)
        s = jnp.cumsum(z, axis=1)
        X_state = Ct * s
        Y = jnp.einsum('bln,dn->bld', Ct * X_state, Wo) + bo
        return Y

    def _L0_ffn_ref(x, ln1_g, ln1_b, w1, b1, ln2_g, ln2_b, w2, b2):
        import jax, jax.numpy as jnp
        import numpy as np
        LN_EPS = 1e-05

        def layer_norm(x, g, b):
            mu = jnp.mean(x, axis=-1, keepdims=True)
            var = jnp.mean(jnp.square(x - mu), axis=-1, keepdims=True)
            return (x - mu) * jax.lax.rsqrt(var + LN_EPS) * g + b

        def ternary_quant(w):
            scale = 1.0 / jnp.clip(jnp.mean(jnp.abs(w)), 1e-05)
            wq = jnp.clip(jnp.round(w * scale), -1.0, 1.0) / scale
            return w + jax.lax.stop_gradient(wq - w)
        h = layer_norm(x, ln1_g, ln1_b)
        h = jnp.einsum('bsd,hd->bsh', h, ternary_quant(w1)) + b1
        h = jax.nn.gelu(h, approximate=False)
        h = layer_norm(h, ln2_g, ln2_b)
        out = jnp.einsum('bsh,dh->bsd', h, ternary_quant(w2)) + b2
        return out
    h = _L0_tok_ref(x, L0_tok_weight, L0_tok_bias)
    h = h + _L0_attn_ref(_layernorm(h, axis=-1), L0_attn_A_log, L0_attn_WB, L0_attn_bB, L0_attn_WC, L0_attn_bC, L0_attn_Wd, L0_attn_bd, L0_attn_Wo, L0_attn_bo)
    h = h + _L0_ffn_ref(_layernorm(h, axis=-1), L0_ffn_ln1_g, L0_ffn_ln1_b, L0_ffn_w1, L0_ffn_b1, L0_ffn_ln2_g, L0_ffn_ln2_b, L0_ffn_w2, L0_ffn_b2)
    return h

_drawn_inputs = setup_inputs


def setup_inputs(seed=0):
    import zlib

    import numpy as np

    out = dict(_drawn_inputs(seed))
    spreads = {'L0_ffn_ln1_g': (1.0, 0.2),
     'L0_ffn_ln1_b': (0.0, 0.1),
     'L0_ffn_b1': (0.0, 0.1),
     'L0_ffn_ln2_g': (1.0, 0.2),
     'L0_ffn_ln2_b': (0.0, 0.1),
     'L0_ffn_b2': (0.0, 0.1)}
    factors = {'L0_attn_bB': 8.0}
    for name, (base, spread) in spreads.items():
        noise = np.random.default_rng([zlib.crc32(name.encode()), seed]).standard_normal(out[name].shape)
        drawn = base * np.exp(spread * noise) if base else spread * noise
        out[name] = jnp.asarray(drawn.astype(out[name].dtype))
    for name, factor in factors.items():
        out[name] = (out[name] * factor).astype(out[name].dtype)
    return out
```

```python
from contextlib import ExitStack

import concourse.bass as bass
from concourse import mybir

ALU = mybir.AluOpType
ACT = mybir.ActivationFunctionType
AX = mybir.AxisListType
F32 = mybir.dt.float32
F16 = mybir.dt.float16
I32 = mybir.dt.int32

P = 128
D = 256
KD = D // P
N = 64
HID = 1024
KH = HID // P
BATCH, SEQ = 8, 2048
TG = 512
TILES = TG // P
UT = 2 * TILES
CHUNKS = SEQ // TG
PAIRS = BATCH // 2
UNITS = PAIRS * CHUNKS
WO = D + 2
TINY = 7

LN_EPS = 1e-5
EPS = 1e-6
XS = 16.0
US = 32.0


class Unit:

    def __init__(self, pair, k):
        self.n = pair * CHUNKS + k
        self.slot = k % CHUNKS
        self.pair = pair + k // CHUNKS


def zero(x):
    return isinstance(x, int) and x == 0


def schedule(eng, stage):
    stage(0, 0, 9)
    with eng.Fori(0, PAIRS - 1) as pair:
        for k in range(1, CHUNKS + 1):
            stage(pair, k, 9)
    for k in range(1, CHUNKS):
        stage(PAIRS - 1, k, CHUNKS - 1 - k)


def lm_tower(nc, tokens, table, tok_bias, a_log, b_bias, d_bias, proj_w, wo_t, bo, ln1_g, ln1_b, w1_t, b1, ln2_g,
             ln2_b, w2_t, b2, out):
    with ExitStack() as ctx:
        def sb(name, shape, dt=F32):
            return ctx.enter_context(nc.sbuf_tensor(name, shape, dt))

        def ps(name):
            return ctx.enter_context(nc.psum_tensor(name, [P, TG], F32))

        def sem(name):
            return ctx.enter_context(nc.semaphore(name))

        ident = sb("ident", [P, P])
        ones = sb("ones", [P, P])
        ones_row = sb("ones_row", [P, TG])
        eps_col = sb("eps_col", [P, 1])
        half = sb("half", [P, UT])
        tok_bias_b = sb("tok_bias_b", [P, D])
        bo_b = sb("bo_b", [P, D])
        b2_b = sb("b2_b", [P, D])
        end_bias_b = sb("end_bias_b", [P, D])
        colsum_b = sb("colsum_b", [P, D])
        proj = sb("proj", [P, KD, 4 * N])
        wo2 = sb("wo2", [P, D])
        t1 = sb("t1", [P, KD, HID], F16)
        t2 = sb("t2", [P, KH, WO], F16)
        absum = sb("absum", [P, 2])
        wscale = sb("wscale", [P, 2])
        winv = sb("winv", [P, 2])
        gelu_scale = sb("gelu_scale", [P, 1])
        alpha_scale = sb("alpha_scale", [P, 1])
        a_col = sb("a_col", [P, 1])
        a_soft = sb("a_soft", [P, 1])
        a_neg = sb("a_neg", [P, 1])
        a_inv = sb("a_inv", [P, 1])
        bb_col = sb("bb_col", [P, 1])
        bd_col = sb("bd_col", [P, 1])
        g1_col = sb("g1_col", [P, KD])
        g1_s = sb("g1_s", [P, KD])
        b1n_col = sb("b1n_col", [P, KD])
        b1_col = sb("b1_col", [P, KH])
        b1_eff = sb("b1_eff", [P, KH])
        g2_col = sb("g2_col", [P, KH])
        b2n_col = sb("b2n_col", [P, KH])
        g2_zero = sb("g2_zero", [P, KH])
        g2_some = sb("g2_some", [P, KH])
        g2_safe = sb("g2_safe", [P, KH])
        g2_s = sb("g2_s", [P, KH])
        g2_inv = sb("g2_inv", [P, KH])

        idx = sb("idx", [P, CHUNKS, UT], I32)
        E = sb("E", [P, CHUNKS, UT, D])
        st1 = sb("st1", [P, UT, 6])
        mv1 = sb("mv1", [P, UT, 2])
        rs1 = sb("rs1", [P, UT])
        xn = sb("xn", [P, UT, D])
        xnT = sb("xnT", [P, KD, 2, TG])
        xb = sb("xb", [P, TG])
        xa = sb("xa", [P, TG])
        delta = sb("delta", [P, TG])
        dsum = sb("dsum", [P, 2, TG + 1])
        dA = sb("dA", [P, TG])
        ct = sb("ct", [P, TG])
        ct2 = sb("ct2", [P, TG])
        lc = sb("lc", [P, TG])
        r0 = sb("r0", [P, TG])
        er = sb("er", [P, TG])
        rn = sb("rn", [P, TG])
        zz = sb("zz", [P, TG])
        ssum = sb("ssum", [P, 2, TG])
        G = sb("G", [P, TG])
        st2 = sb("st2", [P, UT, 6])
        mv2 = sb("mv2", [P, UT, 2])
        rs2 = sb("rs2", [P, UT])
        xn2 = sb("xn2", [P, UT, D])
        x_hi = sb("x_hi", [P, 2, KD, TG], F16)
        x_lo = sb("x_lo", [P, 2, KD, TG], F16)
        gf = sb("gf", [P, KH, TG])
        sq = sb("sq", [P, KH, TG])
        sq4 = sb("sq4", [P, KH // 2, TG])
        sq1 = sb("sq1", [P, TG])
        u_hi = sb("u_hi", [P, 2, KH, TG], F16)
        u_lo = sb("u_lo", [P, 2, KH, TG], F16)
        po = sb("po", [P, TILES, WO])
        s_sum = sb("s_sum", [P, TILES])
        s_mean = sb("s_mean", [P, TILES])
        s_msq = sb("s_msq", [P, TILES])
        s_var = sb("s_var", [P, TILES])
        s_rs = sb("s_rs", [P, TILES])
        s_alpha = sb("s_alpha", [P, TILES])
        s_beta = sb("s_beta", [P, TILES])
        fin = sb("fin", [P, 2, D])
        w1_f, w2_f = [u_lo[:, g, :, :].rearrange("p a b -> p (a b)").bitcast(F32).rearrange("p (k n) -> p k n", k=k)
                      for g, k in ((0, KD), (1, KH))]
        scratch = gf[:, 0:4, :].rearrange("p a b -> p (a b)")
        wide = sq[:, 0:2, :].rearrange("p a b -> p (a b)").rearrange("p (k n) -> p k n", k=KH)
        wide2 = sq[:, 2:4, :].rearrange("p a b -> p (a b)").rearrange("p (k n) -> p k n", k=KH)

        T = [ps("T0"), ps("T1")]
        H = [ps("H0"), ps("H1")]
        O = [ps("O0"), ps("O1")]
        X = [ps("X0"), ps("X1")]
        SQ_PS = O[0][:, 300:300 + TILES]

        small_in = sem("small_in")
        w_in = sem("w_in")
        idx_in = [sem(f"idx_in{c}") for c in range(CHUNKS)]
        gathered = [sem(f"gathered{c}") for c in range(CHUNKS)]
        stored = [sem(f"stored{c}") for c in range(CHUNKS)]
        pool_const = sem("pool_const")
        prep_v = sem("prep_v")
        prep_a = sem("prep_a")
        abs_ps = sem("abs_ps")
        bias_ps = sem("bias_ps")
        h_ready = sem("h_ready")
        st1_done = sem("st1_done")
        mv1_done = sem("mv1_done")
        rs1_sum = sem("rs1_sum")
        rs1_done = sem("rs1_done")
        xn_done = sem("xn_done")
        bo_added = sem("bo_added")
        xt_ps = sem("xt_ps")
        xt_a = sem("xt_a")
        xt_v = sem("xt_v")
        proj_ps = sem("proj_ps")
        xb_done = sem("xb_done")
        xa_done = sem("xa_done")
        delta_done = sem("delta_done")
        carry_done = sem("carry_done")
        dsum_done = sem("dsum_done")
        dA_done = sem("dA_done")
        ct_done = sem("ct_done")
        lc_done = sem("lc_done")
        r0_done = sem("r0_done")
        ct2_done = sem("ct2_done")
        er_done = sem("er_done")
        rn_done = sem("rn_done")
        v_done = sem("v_done")
        z_done = sem("z_done")
        ssum_done = sem("ssum_done")
        g_done = sem("g_done")
        y_ps = sem("y_ps")
        h2_done = sem("h2_done")
        st2_done = sem("st2_done")
        mv2_done = sem("mv2_done")
        rs2_sum = sem("rs2_sum")
        rs2_done = sem("rs2_done")
        xn2_done = sem("xn2_done")
        end_added = sem("end_added")
        x2_ps = sem("x2_ps")
        x_hi_done = sem("x_hi_done")
        x_lo_done = sem("x_lo_done")
        hid_ps = sem("hid_ps")
        gelu_done = sem("gelu_done")
        sq_done = sem("sq_done")
        u_hi_done = sem("u_hi_done")
        u_done = sem("u_done")
        sq_sum = sem("sq_sum")
        o_ps = sem("o_ps")
        po_done = sem("po_done")
        sq_ps = sem("sq_ps")
        tiny = sem("tiny")
        s_rs_done = sem("s_rs_done")
        fin_q = sem("fin_q")
        out_done = sem("out_done")

        held_v, held_p = sem("held_v"), sem("held_p")

        small = [(a_col, a_log), (bb_col, b_bias), (bd_col, d_bias), (g1_col, ln1_g), (b1n_col, ln1_b),
                 (b1_col, b1), (g2_col, ln2_g), (b2n_col, ln2_b), (wo2, wo_t)]
        rows = [(tok_bias_b, tok_bias), (bo_b, bo), (b2_b, b2)]
        SMALL = 16 * (len(small) + len(rows) + 1)

        block = ctx.enter_context(nc.Block())

        @block.sync
        def _(sp):
            def load_idx(v):
                if not zero(v.pair):
                    sp.wait_ge(gathered[v.slot], v.pair * (16 * UT))
                sp.dma_start(idx[:, v.slot, :], tokens[bass.ds(v.pair * CHUNKS + v.slot, 1), :, :].rearrange(
                    "a p t -> (a p) t")).then_inc(idx_in[v.slot], 16)

            def store(v, g):
                sp.wait_ge(out_done, v.n * UT + (g + 1) * TILES)
                dst = out[bass.ds(v.pair * 2 + g, 1), v.slot * TG:(v.slot + 1) * TG, :].rearrange(
                    "a (t p) d -> p (a t) d", p=P)
                sp.dma_start(dst, E[:, v.slot, g * TILES:(g + 1) * TILES, :]).then_inc(stored[v.slot], 16)

            for c in range(CHUNKS - 1):
                load_idx(Unit(0, c))
            sp.dma_start(w1_f[:, :, :], w1_t.rearrange("(k p) n -> p k n", p=P)).then_inc(w_in, 16)
            sp.dma_start(w2_f[:, :, :], w2_t.rearrange("(k p) n -> p k n", p=P)).then_inc(w_in, 16)
            for dst, src in rows:
                sp.dma_start(dst[:, :], src.partition_broadcast(P)).then_inc(small_in, 16)
            for dst, src in small:
                sp.dma_start(dst[:, :], src).then_inc(small_in, 16)
            sp.dma_start(proj[:, :, :], proj_w.rearrange("(k p) n -> p k n", p=P)).then_inc(small_in, 16)

            def stage(pair, k, left):
                if left >= 3:
                    load_idx(Unit(pair, k + 3))
                if k or not zero(pair):
                    store(Unit(pair, k - 1), 1)
                store(Unit(pair, k), 0)

            schedule(sp, stage)
            store(Unit(PAIRS - 1, CHUNKS - 1), 1)
            for c in range(CHUNKS):
                sp.wait_ge(stored[c], 32 * PAIRS)

        @block.gpsimd
        def _(pool):
            nc.gpsimd.memset(ones[:, :], 1.0).then_inc(pool_const, 1)
            nc.gpsimd.memset(ones_row[:, :], 1.0).then_inc(pool_const, 1)
            nc.gpsimd.memset(half[:, :], -0.5).then_inc(pool_const, 1)
            pool.wait_ge(pool_const, 3)
            nc.gpsimd.affine_select(out=ident[:, :], in_=ones[:, :], pattern=[[-1, P]], compare_op=ALU.is_equal,
                                    fill=0.0, base=0, channel_multiplier=1).then_inc(pool_const, 1)

            def gather(v):
                pool.wait_ge(idx_in[v.slot], (v.pair + 1) * 16)
                if not zero(v.pair):
                    pool.wait_ge(stored[v.slot], v.pair * 32)
                pool.sem_inc(held_p, 1)
                for t in range(UT):
                    nc.gpsimd.indirect_dma_start(
                        out=E[:, v.slot, t, :], out_offset=None, in_=table,
                        in_offset=bass.IndirectOffsetOnAxis(ap=idx[:, v.slot, t:t + 1], axis=0),
                    ).then_inc(gathered[v.slot], 16)

            def add_row(v, row):
                return nc.gpsimd.tensor_tensor(E[:, v.slot, :, :], E[:, v.slot, :, :],
                                               row[:, :].unsqueeze(1).broadcast_to([P, UT, D]), ALU.add)

            def embed(v):
                pool.wait_ge(gathered[v.slot], (v.pair + 1) * (16 * UT))
                add_row(v, tok_bias_b).then_inc(h_ready, 1)

            def norm1(v):
                pool.wait_ge(mv1_done, v.n + 1)
                pool.sem_inc(held_p, 1)
                nc.gpsimd.tensor_scalar(rs1[:, :], mv1[:, :, 1], 1.0, LN_EPS, ALU.mult, ALU.add).then_inc(rs1_sum, 1)
                pool.wait_ge(rs1_sum, v.n + 1)
                nc.gpsimd.tensor_tensor(rs1[:, :], rs1[:, :], half[:, :], ALU.pow).then_inc(rs1_done, 1)

            def add_bo(v):
                pool.wait_ge(xn_done, v.n * 2 + 2)
                add_row(v, bo_b).then_inc(bo_added, 1)

            def norm2(v):
                pool.wait_ge(mv2_done, v.n + 1)
                pool.sem_inc(held_p, 1)
                nc.gpsimd.tensor_scalar(rs2[:, :], mv2[:, :, 1], 1.0 + LN_EPS, LN_EPS * LN_EPS, ALU.mult,
                                        ALU.add).then_inc(rs2_sum, 1)
                pool.wait_ge(rs2_sum, v.n + 1)
                nc.gpsimd.tensor_tensor(rs2[:, :], rs2[:, :], half[:, :], ALU.pow).then_inc(rs2_done, 1)

            def add_end(v):
                pool.wait_ge(xn2_done, v.n * 2 + 2)
                add_row(v, end_bias_b).then_inc(end_added, 1)

            def sum_squares(n):
                pool.wait_ge(sq_done, n * KH + KH)
                nc.gpsimd.tensor_tensor(sq4[:, :, :], sq[:, 0:4, :], sq[:, 4:8, :], ALU.add).then_inc(sq_sum, 1)
                pool.wait_ge(sq_sum, n * 3 + 1)
                nc.gpsimd.tensor_tensor(sq4[:, 0:2, :], sq4[:, 0:2, :], sq4[:, 2:4, :], ALU.add).then_inc(sq_sum, 1)
                pool.wait_ge(sq_sum, n * 3 + 2)
                if not zero(n):
                    pool.wait_ge(sq_ps, n)
                nc.gpsimd.tensor_tensor(sq1[:, :], sq4[:, 0, :], sq4[:, 1, :], ALU.add).then_inc(sq_sum, 1)

            def root_hidden(n):
                pool.wait_ge(tiny, n * TINY + 5)
                nc.gpsimd.tensor_tensor(s_rs[:, :], s_var[:, :], half[:, 0:TILES], ALU.pow).then_inc(s_rs_done, 1)

            for c in range(3):
                gather(Unit(0, c))
            pool.wait_ge(pool_const, 4)
            pool.wait_ge(small_in, SMALL)
            embed(Unit(0, 0))
            norm1(Unit(0, 0))
            add_bo(Unit(0, 0))
            embed(Unit(0, 1))
            norm2(Unit(0, 0))
            add_end(Unit(0, 0))
            norm1(Unit(0, 1))
            add_bo(Unit(0, 1))

            def stage(pair, k, left):
                n = Unit(pair, k).n
                if not zero(n):
                    root_hidden(n * 2 - 1)
                if left >= 2:
                    embed(Unit(pair, k + 2))
                sum_squares(n * 2)
                if left >= 3:
                    gather(Unit(pair, k + 3))
                if left >= 2:
                    norm1(Unit(pair, k + 2))
                root_hidden(n * 2)
                if left >= 1:
                    norm2(Unit(pair, k + 1))
                sum_squares(n * 2 + 1)
                if left >= 1:
                    add_end(Unit(pair, k + 1))
                if left >= 2:
                    add_bo(Unit(pair, k + 2))

            schedule(pool, stage)
            root_hidden(UNITS * 2 - 1)

        @block.scalar
        def _(act):
            def copy_xt(v):
                for h in range(2):
                    act.wait_ge(xt_ps, v.n * 2 + (h + 1))
                    if not zero(v.n):
                        act.wait_ge(proj_ps, v.n)
                    nc.scalar.copy(xnT[:, 0, h, :], T[0][:, :]).then_inc(xt_a, 1)

            def softplus_part(v):
                act.wait_ge(proj_ps, v.n + 1)
                if not zero(v.n):
                    act.wait_ge(delta_done, v.n)
                nc.scalar.activation(xb[0:N, :], X[0][N:P, :], ACT.Identity, bias=bd_col[N:P, :]).then_inc(xb_done, 1)
                nc.scalar.activation(xb[N:P, :], X[1][0:N, :], ACT.Identity, bias=bd_col[0:N, :]).then_inc(xb_done, 1)
                act.wait_ge(xb_done, v.n * 2 + 2)
                nc.scalar.activation(xa[:, :], xb[:, :], ACT.Abs).then_inc(xa_done, 1)
                act.wait_ge(xa_done, v.n * 3 + 1)
                nc.scalar.activation(xa[:, :], xa[:, :], ACT.Exp, scale=-1.0).then_inc(xa_done, 1)
                act.wait_ge(xa_done, v.n * 3 + 2)
                nc.scalar.activation(xa[:, :], xa[:, :], ACT.Ln, bias=1.0).then_inc(xa_done, 1)

            def decay_part(v):
                act.wait_ge(delta_done, v.n + 1)
                if not zero(v.n):
                    act.wait_ge(v_done, v.n)
                nc.scalar.activation(dA[:, :], delta[:, :], ACT.Exp, scale=a_neg[:, :]).then_inc(dA_done, 1)
                act.wait_ge(dsum_done, v.n + 1)
                if not zero(v.n):
                    act.wait_ge(er_done, v.n)
                nc.scalar.activation(ct[:, :], dsum[:, v.slot % 2, 0:TG], ACT.Exp, scale=a_neg[:, :]).then_inc(ct_done, 1)
                act.wait_ge(ct_done, v.n + 1)
                nc.scalar.activation(lc[:, :], ct[:, :], ACT.Ln, bias=eps_col[:, :]).then_inc(lc_done, 1)
                act.wait_ge(lc_done, v.n + 1)
                if not zero(v.n):
                    act.wait_ge(rn_done, v.n)
                nc.scalar.activation(r0[:, :], lc[:, :], ACT.Exp, scale=-1.0).then_inc(r0_done, 1)
                if not zero(v.n):
                    act.wait_ge(g_done, v.n)
                nc.scalar.activation(ct2[:, :], ct[:, :], ACT.Square).then_inc(ct2_done, 1)

            def high_x(v, g):
                n = v.n * 2 + g
                act.wait_ge(x2_ps, n + 1)
                if not zero(v.n):
                    act.wait_ge(hid_ps, (n - 1) * KH)
                for k in range(KD):
                    nc.scalar.activation(x_hi[:, g, k, :], T[k][:, :], ACT.Identity,
                                         scale=g1_s[:, k:k + 1]).then_inc(x_hi_done, 1)

            def gelu(v, g):
                n = v.n * 2 + g

                def square(m):
                    act.wait_ge(gelu_done, n * KH + (m + 1))
                    nc.scalar.activation(sq[:, m, :], gf[:, m, :], ACT.Square).then_inc(sq_done, 1)

                for m in range(KH):
                    act.wait_ge(hid_ps, n * KH + (m + 1))
                    if not zero(n):
                        act.wait_ge(u_done, n * KH + (m + 1 - KH))
                        act.wait_ge(sq_done, n * KH + (m + 1 - KH))
                    nc.scalar.activation(gf[:, m, :], H[m % 2][:, :], ACT.Gelu, scale=gelu_scale[:, :],
                                         bias=b1_eff[:, m:m + 1]).then_inc(gelu_done, 1)
                    if m == 0 and not zero(n):
                        act.wait_ge(sq_sum, n * 3 - 2)
                    if m:
                        square(m - 1)
                square(KH - 1)

            def copy_out(v, g, t):
                n = v.n * 2 + g
                act.wait_ge(o_ps, n * TILES + (t + 1))
                if not zero(n):
                    act.wait_ge(out_done, n * TILES + (t + 1 - TILES))
                nc.scalar.copy(po[:, t, :], O[t % 2][:, 0:WO]).then_inc(po_done, 1)

            nc.scalar.preload_act_table_set("natural_log_exp_and_others")
            act.wait_ge(small_in, SMALL)
            nc.scalar.activation(a_soft[:, :], a_col[:, :], ACT.Abs).then_inc(prep_a, 1)
            act.wait_ge(prep_a, 1)
            nc.scalar.activation(a_soft[:, :], a_soft[:, :], ACT.Exp, scale=-1.0).then_inc(prep_a, 1)
            act.wait_ge(prep_a, 2)
            nc.scalar.activation(a_soft[:, :], a_soft[:, :], ACT.Ln, bias=1.0).then_inc(prep_a, 1)
            copy_xt(Unit(0, 0))
            softplus_part(Unit(0, 0))
            decay_part(Unit(0, 0))

            def stage(pair, k, left):
                u, after = Unit(pair, k), Unit(pair, k + 1)
                high_x(u, 0)
                if left >= 1:
                    copy_xt(after)
                gelu(u, 0)
                if left >= 1:
                    nc.scalar.preload_act_table_set("natural_log_exp_and_others")
                    softplus_part(after)
                copy_out(u, 0, 0)
                copy_out(u, 0, 1)
                if left >= 1:
                    decay_part(after)
                copy_out(u, 0, 2)
                copy_out(u, 0, 3)
                high_x(u, 1)
                gelu(u, 1)
                for t in range(TILES):
                    copy_out(u, 1, t)

            schedule(act, stage)

        @block.vector
        def _(dve):
            steps = [0]

            def link(ins):
                steps[0] += 1
                ins.then_inc(prep_v, 1)
                dve.wait_ge(prep_v, steps[0])

            dve.wait_ge(w_in, 32)
            link(nc.vector.memset(eps_col[:, :], EPS))
            link(nc.vector.tensor_reduce(absum[:, 0:1], w1_f[:, :, :], AX.XY, ALU.add, apply_absolute_value=True))
            link(nc.vector.tensor_reduce(absum[:, 1:2], w2_f[:, :, :], AX.XY, ALU.add, apply_absolute_value=True))
            assert steps[0] == ABSUM_STEPS
            dve.wait_ge(abs_ps, 1)
            link(nc.vector.tensor_scalar(wscale[:, :], X[0][:, 0:2], 1.0 / (D * HID), 1e-5, ALU.mult, ALU.max))
            link(nc.vector.reciprocal(winv[:, :], wscale[:, :]))
            link(nc.vector.tensor_scalar(gelu_scale[:, :], wscale[:, 0:1], 1.0 / XS, None, ALU.mult))
            link(nc.vector.tensor_scalar(alpha_scale[:, :], wscale[:, 1:2], 1.0 / US, None, ALU.mult))
            for i, (w, c) in enumerate(((w1_f, KD), (w2_f, KH))):
                flat = w.rearrange("p a b -> p (a b)")
                link(nc.vector.tensor_scalar(scratch, flat, winv[:, i:i + 1], 0.5, ALU.mult, ALU.is_gt))
                link(nc.vector.tensor_scalar(flat, flat, winv[:, i:i + 1], -0.5, ALU.mult, ALU.is_lt))
                link(nc.vector.tensor_tensor(flat, scratch, flat, ALU.subtract))
            link(nc.vector.tensor_copy(t1[:, :, :], w1_f[:, :, :]))
            dve.wait_ge(small_in, SMALL)
            link(nc.vector.tensor_scalar(g2_zero[:, :], g2_col[:, :], 0.0, None, ALU.is_equal))
            link(nc.vector.tensor_scalar(g2_some[:, :], g2_zero[:, :], -1.0, 1.0, ALU.mult, ALU.add))
            link(nc.vector.tensor_tensor(g2_safe[:, :], g2_col[:, :], g2_zero[:, :], ALU.add))
            link(nc.vector.tensor_scalar(g2_s[:, :], g2_safe[:, :], US, None, ALU.mult))
            link(nc.vector.reciprocal(g2_inv[:, :], g2_safe[:, :]))
            for k in range(KH):
                link(nc.vector.tensor_scalar(t2[:, k, 0:D], w2_f[:, k, :], g2_some[:, k:k + 1], None, ALU.mult))
            link(nc.vector.tensor_copy(t2[:, :, D], g2_inv[:, :]))
            link(nc.vector.tensor_tensor(t2[:, :, D + 1], g2_inv[:, :], t2[:, :, D], ALU.subtract))
            link(nc.vector.tensor_copy(wide, g2_col[:, :].unsqueeze(2).broadcast_to([P, KH, P])))
            link(nc.vector.tensor_copy(wide2, b2n_col[:, :].unsqueeze(2).broadcast_to([P, KH, P])))
            assert steps[0] == WIDE_STEPS
            link(nc.vector.tensor_scalar(g1_s[:, :], g1_col[:, :], XS, None, ALU.mult))
            dve.wait_ge(prep_a, 3)
            link(nc.vector.scalar_tensor_tensor(a_neg[:, :], a_col[:, :], 0.0, a_soft[:, :], ALU.max, ALU.add))
            link(nc.vector.tensor_scalar(a_neg[:, :], a_neg[:, :], -1.0, None, ALU.mult))
            link(nc.vector.tensor_scalar(a_inv[:, :], a_neg[:, :], EPS, -1.0, ALU.add, ALU.mult))
            link(nc.vector.reciprocal(a_inv[:, :], a_inv[:, :]))
            dve.wait_ge(bias_ps, 1)
            link(nc.vector.scalar_tensor_tensor(b1_eff[:, :], T[0][:, 0:KH], wscale[:, 0:1], b1_col[:, :], ALU.mult,
                                                ALU.add))
            link(nc.vector.tensor_copy(colsum_b[:, :], X[0][:, 0:D]))
            link(nc.vector.scalar_tensor_tensor(end_bias_b[:, :], X[1][:, 0:D], wscale[:, 1:2], b2_b[:, :], ALU.mult,
                                                ALU.add))
            assert steps[0] == PREP_STEPS
            dve.wait_ge(pool_const, 4)

            def stats(v, st, mv, st_done, mv_done):
                for t in range(UT):
                    last = nc.vector.bn_stats(st[:, t, :], E[:, v.slot, t, :])
                last.then_inc(st_done, 1)
                dve.wait_ge(st_done, v.n + 1)
                dve.sem_inc(held_v, 1)
                for t in range(UT):
                    last = nc.vector.bn_aggr(mv[:, t, :], st[:, t, :])
                last.then_inc(mv_done, 1)

            def normalise(v, dst, mv, rs, done):
                for t in range(UT):
                    last = nc.vector.tensor_scalar(dst[:, t, :], E[:, v.slot, t, :], mv[:, t, 0:1], rs[:, t:t + 1],
                                                   ALU.subtract, ALU.mult)
                    if t % TILES == TILES - 1:
                        last.then_inc(done, 1)

            def stats1(v):
                dve.wait_ge(h_ready, v.n + 1)
                stats(v, st1, mv1, st1_done, mv1_done)

            def normalise1(v):
                dve.wait_ge(rs1_done, v.n + 1)
                if not zero(v.n):
                    dve.wait_ge(xt_ps, v.n * 2)
                normalise(v, xn, mv1, rs1, xn_done)

            def copy_xt(v):
                for h in range(2):
                    dve.wait_ge(xt_ps, v.n * 2 + (h + 1))
                    if not zero(v.n):
                        dve.wait_ge(proj_ps, v.n)
                    nc.vector.tensor_copy(xnT[:, 1, h, :], T[1][:, :]).then_inc(xt_v, 1)

            def recurrence(v):
                b = v.slot % 2
                dve.wait_ge(xa_done, v.n * 3 + 3)
                if not zero(v.n):
                    dve.wait_ge(dA_done, v.n)
                nc.vector.scalar_tensor_tensor(delta[:, :], xb[:, :], 0.0, xa[:, :], ALU.max, ALU.add).then_inc(delta_done, 1)
                if not zero(v.n):
                    dve.wait_ge(ct_done, v.n)
                if v.slot == 0:
                    nc.vector.memset(dsum[:, b, 0:1], 0.0).then_inc(carry_done, 1)
                else:
                    dve.wait_ge(dsum_done, v.n)
                    nc.vector.tensor_copy(dsum[:, b, 0:1], dsum[:, 1 - b, TG:TG + 1]).then_inc(carry_done, 1)
                dve.wait_ge(delta_done, v.n + 1)
                dve.wait_ge(carry_done, v.n + 1)
                nc.vector.tensor_tensor_scan(dsum[:, b, 1:TG + 1], ones_row[:, :], delta[:, :], dsum[:, b, 0:1],
                                             ALU.mult, ALU.add).then_inc(dsum_done, 1)
                dve.wait_ge(r0_done, v.n + 1)
                nc.vector.scalar_tensor_tensor(er[:, :], ct[:, :], EPS, r0[:, :], ALU.add, ALU.mult).then_inc(er_done, 1)
                dve.wait_ge(er_done, v.n + 1)
                nc.vector.scalar_tensor_tensor(rn[:, :], er[:, :], -2.0, r0[:, :], ALU.add, ALU.mult).then_inc(rn_done, 1)
                dve.wait_ge(rn_done, v.n + 1)
                nc.vector.scalar_tensor_tensor(zz[:, :], dA[:, :], -1.0, rn[:, :], ALU.add, ALU.mult).then_inc(v_done, 1)
                dve.wait_ge(v_done, v.n + 1)
                nc.vector.scalar_tensor_tensor(zz[0:N, :], X[0][0:N, :], bb_col[0:N, :], zz[0:N, :], ALU.add,
                                               ALU.mult).then_inc(z_done, 1)
                nc.vector.scalar_tensor_tensor(zz[N:P, :], X[1][N:P, :], bb_col[N:P, :], zz[N:P, :], ALU.add,
                                               ALU.mult).then_inc(z_done, 1)
                dve.wait_ge(z_done, v.n * 2 + 2)
                if v.slot:
                    dve.wait_ge(ssum_done, v.n)
                nc.vector.tensor_tensor_scan(ssum[:, b, :], ones_row[:, :], zz[:, :],
                                             ssum[:, 1 - b, TG - 1:TG] if v.slot else 0.0,
                                             ALU.mult, ALU.add).then_inc(ssum_done, 1)
                dve.wait_ge(ssum_done, v.n + 1)
                dve.wait_ge(ct2_done, v.n + 1)
                if not zero(v.n):
                    dve.wait_ge(y_ps, v.n * 4)
                nc.vector.scalar_tensor_tensor(G[:, :], ssum[:, b, :], a_inv[:, :], ct2[:, :], ALU.mult,
                                               ALU.mult).then_inc(g_done, 1)

            def residual(v):
                dve.wait_ge(bo_added, v.n + 1)
                for q in range(4):
                    dve.wait_ge(y_ps, v.n * 4 + (q + 1))
                    e = E[:, v.slot, 2 * q:2 * q + 2, :].rearrange("p t d -> p (t d)")
                    nc.vector.tensor_tensor(e, X[q % 2][:, :], e, ALU.add).then_inc(h2_done, 1)

            def stats2(v):
                dve.wait_ge(h2_done, v.n * 4 + 4)
                stats(v, st2, mv2, st2_done, mv2_done)

            def normalise2(v):
                dve.wait_ge(rs2_done, v.n + 1)
                if not zero(v.n):
                    dve.wait_ge(x2_ps, v.n * 2)
                normalise(v, xn2, mv2, rs2, xn2_done)

            def low_x(v, g):
                n = v.n * 2 + g
                if not zero(v.n):
                    dve.wait_ge(hid_ps, (n - 1) * KH)
                for k in range(KD):
                    dve.wait_ge(x_hi_done, n * 2 + (k + 1))
                    nc.vector.scalar_tensor_tensor(x_lo[:, g, k, :], T[k][:, :], g1_s[:, k:k + 1], x_hi[:, g, k, :],
                                                   ALU.mult, ALU.subtract).then_inc(x_lo_done, 1)

            def step(n, i, ins):
                ins.then_inc(tiny, 1)
                dve.wait_ge(tiny, n * TINY + i)

            def hidden_variance(n):
                dve.wait_ge(po_done, n * TILES + TILES)
                step(n, 1, nc.vector.tensor_tensor(s_sum[:, :], po[:, :, D], po[:, :, D + 1], ALU.add))
                step(n, 2, nc.vector.tensor_scalar(s_mean[:, :], s_sum[:, :], 1.0 / (US * HID), None, ALU.mult))
                step(n, 3, nc.vector.tensor_tensor(s_msq[:, :], s_mean[:, :], s_mean[:, :], ALU.mult))
                dve.wait_ge(sq_ps, n + 1)
                step(n, 4, nc.vector.scalar_tensor_tensor(s_var[:, :], SQ_PS, 1.0 / HID, s_msq[:, :], ALU.mult,
                                                          ALU.subtract))
                step(n, 5, nc.vector.tensor_scalar(s_var[:, :], s_var[:, :], 0.0, LN_EPS, ALU.max, ALU.add))

            def hidden_scales(n):
                dve.wait_ge(s_rs_done, n + 1)
                step(n, 6, nc.vector.tensor_scalar(s_alpha[:, :], s_rs[:, :], alpha_scale[:, :], None, ALU.mult))
                step(n, 7, nc.vector.scalar_tensor_tensor(s_beta[:, :], s_mean[:, :], -US, s_alpha[:, :], ALU.mult,
                                                          ALU.mult))

            def finish(v, g, t):
                n = v.n * 2 + g
                e = E[:, v.slot, g * TILES + t, :]
                dve.wait_ge(end_added, v.n + 1)
                nc.vector.scalar_tensor_tensor(fin[:, t % 2, :], colsum_b[:, :], s_beta[:, t:t + 1], e, ALU.mult,
                                               ALU.add).then_inc(fin_q, 1)
                dve.wait_ge(fin_q, n * TILES + (t + 1))
                nc.vector.scalar_tensor_tensor(e, po[:, t, 0:D], s_alpha[:, t:t + 1], fin[:, t % 2, :], ALU.mult,
                                               ALU.add).then_inc(out_done, 1)

            def split_hidden(v, g, before):
                n = v.n * 2 + g
                for m in range(KH):
                    dve.wait_ge(gelu_done, n * KH + (m + 1))
                    if m == 0 and not zero(v.n):
                        dve.wait_ge(o_ps, (n - 1) * TILES)
                    nc.vector.tensor_scalar(u_hi[:, g, m, :], gf[:, m, :], g2_s[:, m:m + 1], None,
                                            ALU.mult).then_inc(u_hi_done, 1)
                    dve.wait_ge(u_hi_done, n * KH + (m + 1))
                    nc.vector.scalar_tensor_tensor(u_lo[:, g, m, :], gf[:, m, :], g2_s[:, m:m + 1], u_hi[:, g, m, :],
                                                   ALU.mult, ALU.subtract).then_inc(u_done, 1)
                    if before is not None:
                        if m == 1:
                            hidden_variance(n - 1)
                        if m == 3:
                            hidden_scales(n - 1)
                        if m >= TILES:
                            finish(before, 1 - g, m - TILES)

            first = Unit(0, 0)
            stats1(first)
            normalise1(first)
            copy_xt(first)
            recurrence(first)
            residual(first)
            stats2(first)
            normalise2(first)
            stats1(Unit(0, 1))
            normalise1(Unit(0, 1))

            def stage(pair, k, left):
                u, after, then = Unit(pair, k), Unit(pair, k + 1), Unit(pair, k + 2)
                low_x(u, 0)
                if left >= 1:
                    copy_xt(after)
                split_hidden(u, 0, None if zero(u.n) else Unit(pair, k - 1))
                if left >= 1:
                    recurrence(after)
                if left >= 2:
                    stats1(then)
                low_x(u, 1)
                split_hidden(u, 1, u)
                if left >= 1:
                    residual(after)
                    stats2(after)
                if left >= 2:
                    normalise1(then)
                if left >= 1:
                    normalise2(after)

            schedule(dve, stage)
            last, n = Unit(PAIRS - 1, CHUNKS - 1), UNITS * 2 - 1
            hidden_variance(n)
            hidden_scales(n)
            for t in range(TILES):
                finish(last, 1, t)

        @block.tensor
        def _(pe):
            pe.wait_ge(pool_const, 4)
            pe.wait_ge(prep_v, ABSUM_STEPS)
            nc.tensor.matmul(X[0][:, 0:2], ones[:, :], absum[:, :], start=True, stop=True).then_inc(abs_ps, 1)
            pe.wait_ge(prep_v, WIDE_STEPS)
            for m in range(KH):
                for k in range(KD):
                    nc.tensor.matmul(T[0][:, m:m + 1], w1_f[:, k, m * P:(m + 1) * P], b1n_col[:, k:k + 1],
                                     start=(k == 0), stop=(k == KD - 1))
            for w, x in ((wide, X[0]), (wide2, X[1])):
                for k in range(KH):
                    last = nc.tensor.matmul(x[:, 0:D], w[:, k, :], w2_f[:, k, :], start=(k == 0), stop=(k == KH - 1))
            last.then_inc(bias_ps, 1)
            pe.wait_ge(prep_v, PREP_STEPS)

            def turn_embeddings(v, h):
                pe.wait_ge(xn_done, v.n * 2 + (h + 1))
                if h == 0:
                    if not zero(v.n):
                        pe.wait_ge(x_hi_done, v.n * 4 - 2)
                        pe.wait_ge(x_lo_done, v.n * 4 - 2)
                else:
                    pe.wait_ge(xt_a, v.n * 2 + 1)
                    pe.wait_ge(xt_v, v.n * 2 + 1)
                for k in range(KD):
                    for t in range(TILES):
                        last = nc.tensor.transpose(T[k][:, t * P:(t + 1) * P], xn[:, h * TILES + t, k * P:(k + 1) * P],
                                                   ident[:, :])
                last.then_inc(xt_ps, 1)

            def project(v):
                pe.wait_ge(xt_a, v.n * 2 + 2)
                pe.wait_ge(xt_v, v.n * 2 + 2)
                if not zero(v.n):
                    pe.wait_ge(h2_done, v.n * 4)
                for h in range(2):
                    for k in range(KD):
                        last = nc.tensor.matmul(X[h][:, :], proj[:, k, h * P:(h + 1) * P], xnT[:, k, h, :],
                                                start=(k == 0), stop=(k == KD - 1))
                last.then_inc(proj_ps, 1)

            def attention_out(v):
                pe.wait_ge(g_done, v.n + 1)
                for q in range(4):
                    h = q // 2
                    if q >= 2:
                        pe.wait_ge(h2_done, v.n * 4 + (q - 1))
                    for i in range(2):
                        t = (q % 2) * 2 + i
                        last = nc.tensor.matmul(X[q % 2][:, i * D:(i + 1) * D], G[h * N:(h + 1) * N, t * P:(t + 1) * P],
                                                wo2[h * N:(h + 1) * N, :], start=True, stop=True)
                    last.then_inc(y_ps, 1)

            def turn_stream(v, g):
                pe.wait_ge(xn2_done, v.n * 2 + (g + 1))
                if g == 0:
                    if not zero(v.n):
                        pe.wait_ge(x_hi_done, v.n * 4)
                        pe.wait_ge(x_lo_done, v.n * 4)
                    else:
                        pe.wait_ge(xt_a, 2)
                        pe.wait_ge(xt_v, 2)
                for k in range(KD):
                    for t in range(TILES):
                        last = nc.tensor.transpose(T[k][:, t * P:(t + 1) * P], xn2[:, g * TILES + t, k * P:(k + 1) * P],
                                                   ident[:, :])
                last.then_inc(x2_ps, 1)

            def square_sums(n):
                pe.wait_ge(sq_sum, n * 3 + 3)
                pe.wait_ge(po_done, n * TILES + 3)
                for t in range(TILES):
                    last = nc.tensor.matmul(SQ_PS[:, t:t + 1], sq1[:, t * P:(t + 1) * P], ones[:, 0:1], start=True,
                                            stop=True)
                last.then_inc(sq_ps, 1)

            def first_product(v, g):
                n = v.n * 2 + g
                pe.wait_ge(x_hi_done, n * 2 + 2)
                pe.wait_ge(x_lo_done, n * 2 + 2)
                for m in range(KH):
                    if not (zero(n) and m < 2):
                        pe.wait_ge(gelu_done, n * KH + (m - 1))
                    for k in range(KD):
                        for x in (x_hi, x_lo):
                            last = nc.tensor.matmul(H[m % 2][:, :], t1[:, k, m * P:(m + 1) * P], x[:, g, k, :],
                                                    start=(k == 0 and x is x_hi), stop=(k == KD - 1 and x is x_lo))
                    last.then_inc(hid_ps, 1)

            def second_product(v, g):
                n = v.n * 2 + g
                if not zero(n):
                    pe.wait_ge(tiny, n * TINY - 3)
                for t in range(TILES):
                    if not (zero(n) and t < 2):
                        pe.wait_ge(po_done, n * TILES + (t - 1))
                    for k in range(KH):
                        if t == 0:
                            pe.wait_ge(u_done, n * KH + (k + 1))
                        for x in (u_hi, u_lo):
                            last = nc.tensor.matmul(O[t % 2][:, 0:WO], x[:, g, k, t * P:(t + 1) * P], t2[:, k, :],
                                                    start=(k == 0 and x is u_hi), stop=(k == KH - 1 and x is u_lo))
                    last.then_inc(o_ps, 1)

            first = Unit(0, 0)
            for h in range(2):
                turn_embeddings(first, h)
            project(first)
            attention_out(first)

            def stage(pair, k, left):
                u, after = Unit(pair, k), Unit(pair, k + 1)
                turn_stream(u, 0)
                if left >= 1:
                    for h in range(2):
                        turn_embeddings(after, h)
                    project(after)
                if not zero(u.n):
                    square_sums(u.n * 2 - 1)
                first_product(u, 0)
                second_product(u, 0)
                if left >= 1:
                    pe.wait_ge(xt_a, after.n * 2 + 2)
                    pe.wait_ge(xt_v, after.n * 2 + 2)
                else:
                    pe.wait_ge(x_hi_done, u.n * 4 + 2)
                    pe.wait_ge(x_lo_done, u.n * 4 + 2)
                turn_stream(u, 1)
                square_sums(u.n * 2)
                first_product(u, 1)
                if left >= 1:
                    attention_out(after)
                second_product(u, 1)

            schedule(pe, stage)
            square_sums(UNITS * 2 - 1)


ABSUM_STEPS = 3
WIDE_STEPS = 3 + 4 + 6 + 1 + 5 + KH + 4
PREP_STEPS = WIDE_STEPS + 1 + 4 + 3


def kernel(x, L0_tok_weight, L0_tok_bias, L0_attn_A_log, L0_attn_WB, L0_attn_bB, L0_attn_WC, L0_attn_bC, L0_attn_Wd,
           L0_attn_bd, L0_attn_Wo, L0_attn_bo, L0_ffn_ln1_g, L0_ffn_ln1_b, L0_ffn_w1, L0_ffn_b1, L0_ffn_ln2_g,
           L0_ffn_ln2_b, L0_ffn_w2, L0_ffn_b2):
    import numpy as np
    import concourse.bacc as bacc
    from concourse.bass_utils import run_bass_kernel_spmd

    def twice(a):
        return np.concatenate([a, a]).reshape(P, 1)

    def column(a):
        return np.ascontiguousarray(np.asarray(a).reshape(-1, P).T)

    wb, wd = np.asarray(L0_attn_WB).T, np.repeat(np.asarray(L0_attn_Wd).T, N, axis=1)
    wo = np.asarray(L0_attn_Wo).T
    arrays = {
        "tokens": np.ascontiguousarray(np.asarray(x).reshape(PAIRS, 2, CHUNKS, TILES, P).transpose(0, 2, 4, 1, 3)
                                       .reshape(UNITS, P, UT)),
        "table": np.ascontiguousarray(np.asarray(L0_tok_weight).T),
        "tok_bias": np.asarray(L0_tok_bias),
        "a_log": twice(np.asarray(L0_attn_A_log)),
        "b_bias": twice(np.asarray(L0_attn_bB)),
        "d_bias": np.repeat(np.asarray(L0_attn_bd), P).reshape(P, 1),
        "proj_w": np.ascontiguousarray(np.concatenate([wb, wd, wd, wb], axis=1)),
        "wo_t": np.ascontiguousarray(np.concatenate([wo, wo])),
        "bo": np.asarray(L0_attn_bo),
        "ln1_g": column(L0_ffn_ln1_g),
        "ln1_b": column(L0_ffn_ln1_b),
        "w1_t": np.ascontiguousarray(np.asarray(L0_ffn_w1).T),
        "b1": column(L0_ffn_b1),
        "ln2_g": column(L0_ffn_ln2_g),
        "ln2_b": column(L0_ffn_ln2_b),
        "w2_t": np.ascontiguousarray(np.asarray(L0_ffn_w2).T),
        "b2": np.asarray(L0_ffn_b2),
    }
    nc = bacc.Bacc("TRN2", target_bir_lowering=False, num_devices=1)
    given = {k: nc.dram_tensor(k, a.shape, mybir.dt.from_np(a.dtype), kind="ExternalInput").ap()
             for k, a in arrays.items()}
    out = nc.dram_tensor("out", (BATCH, SEQ, D), F32, kind="ExternalOutput").ap()
    lm_tower(nc, out=out, **given)
    return run_bass_kernel_spmd(nc, [arrays], core_ids=[0]).results[0]["out"]
```

```python
from contextlib import ExitStack

import concourse.bass as bass
from concourse import mybir

ALU = mybir.AluOpType
ACT = mybir.ActivationFunctionType
AX = mybir.AxisListType
F32 = mybir.dt.float32
F16 = mybir.dt.float16
BF16 = mybir.dt.bfloat16
I32 = mybir.dt.int32

P = 128
D = 256
KD = D // P
N = 64
HID = 1024
KH = HID // P
BATCH, SEQ = 8, 2048
TG = 512
TILES = TG // P
UT = 2 * TILES
CHUNKS = SEQ // TG
PAIRS = BATCH // 2
UNITS = PAIRS * CHUNKS
WO = D + 2
TINY = 7

LN_EPS = 1e-5
EPS = 1e-6
XS = 16.0
US = 32.0


class Unit:

    def __init__(self, pair, k):
        self.n = pair * CHUNKS + k
        self.slot = k % CHUNKS
        self.pair = pair + k // CHUNKS


def zero(x):
    return isinstance(x, int) and x == 0


def schedule(eng, stage):
    stage(0, 0, 9)
    with eng.Fori(0, PAIRS - 1) as pair:
        for k in range(1, CHUNKS + 1):
            stage(pair, k, 9)
    for k in range(1, CHUNKS):
        stage(PAIRS - 1, k, CHUNKS - 1 - k)


def lm_tower(nc, tokens, table, tok_bias, a_log, b_bias, d_bias, proj_w, wo_t, bo, ln1_g, ln1_b, w1_t, b1, ln2_g,
             ln2_b, w2_t, b2, out):
    with ExitStack() as ctx:
        def sb(name, shape, dt=F32):
            return ctx.enter_context(nc.sbuf_tensor(name, shape, dt))

        def ps(name):
            return ctx.enter_context(nc.psum_tensor(name, [P, TG], F32))

        def sem(name):
            return ctx.enter_context(nc.semaphore(name))

        ident = sb("ident", [P, P])
        ones = sb("ones", [P, P])
        ones_row = sb("ones_row", [P, TG])
        eps_col = sb("eps_col", [P, 1])
        half = sb("half", [P, UT])
        tok_bias_b = sb("tok_bias_b", [P, D])
        bo_b = sb("bo_b", [P, D])
        ones_bf = sb("ones_bf", [P, P], BF16)
        bo_parts = sb("bo_parts", [P, 2, D], BF16)
        bo_hi = sb("bo_hi", [P, D], BF16)
        bo_rest = sb("bo_rest", [P, D])
        b2_b = sb("b2_b", [P, D])
        end_bias_b = sb("end_bias_b", [P, D])
        colsum_b = sb("colsum_b", [P, D])
        proj = sb("proj", [P, KD, 4 * N])
        wo2 = sb("wo2", [P, D])
        t1 = sb("t1", [P, KD, HID], F16)
        t2 = sb("t2", [P, KH, WO], F16)
        absum = sb("absum", [P, 2])
        wscale = sb("wscale", [P, 2])
        winv = sb("winv", [P, 2])
        gelu_scale = sb("gelu_scale", [P, 1])
        alpha_scale = sb("alpha_scale", [P, 1])
        a_col = sb("a_col", [P, 1])
        a_soft = sb("a_soft", [P, 1])
        a_neg = sb("a_neg", [P, 1])
        a_inv = sb("a_inv", [P, 1])
        bb_col = sb("bb_col", [P, 1])
        bd_col = sb("bd_col", [P, 1])
        g1_col = sb("g1_col", [P, KD])
        g1_s = sb("g1_s", [P, KD])
        b1n_col = sb("b1n_col", [P, KD])
        b1_col = sb("b1_col", [P, KH])
        b1_eff = sb("b1_eff", [P, KH])
        g2_col = sb("g2_col", [P, KH])
        b2n_col = sb("b2n_col", [P, KH])
        g2_zero = sb("g2_zero", [P, KH])
        g2_some = sb("g2_some", [P, KH])
        g2_safe = sb("g2_safe", [P, KH])
        g2_s = sb("g2_s", [P, KH])
        g2_inv = sb("g2_inv", [P, KH])

        idx = sb("idx", [P, CHUNKS, UT], I32)
        E = sb("E", [P, CHUNKS, UT, D])
        st1 = sb("st1", [P, UT, 6])
        mv1 = sb("mv1", [P, UT, 2])
        nm1 = sb("nm1", [P, UT])
        nb1 = sb("nb1", [P, UT])
        rs1 = sb("rs1", [P, UT])
        xn = sb("xn", [P, UT, D])
        xnT = sb("xnT", [P, KD, 2, TG])
        xb = sb("xb", [P, TG])
        xa = sb("xa", [P, TG])
        bt = sb("bt", [P, TG])
        delta = sb("delta", [P, TG])
        dsum = sb("dsum", [P, 2, TG + 1])
        dA = sb("dA", [P, TG])
        ct = sb("ct", [P, TG])
        ct2 = sb("ct2", [P, TG])
        lc = sb("lc", [P, TG])
        r0 = sb("r0", [P, TG])
        er = sb("er", [P, TG])
        rn = sb("rn", [P, TG])
        zz = sb("zz", [P, TG])
        ssum = sb("ssum", [P, 2, TG])
        G = sb("G", [P, TG])
        st2 = sb("st2", [P, UT, 6])
        mv2 = sb("mv2", [P, UT, 2])
        rs2 = sb("rs2", [P, UT])
        xn2 = sb("xn2", [P, UT, D])
        x_hi = sb("x_hi", [P, 2, KD, TG], F16)
        x_lo = sb("x_lo", [P, 2, KD, TG], F16)
        gf = sb("gf", [P, KH, TG])
        sq = sb("sq", [P, KH, TG])
        sq4 = sb("sq4", [P, KH // 2, TG])
        sq1 = sb("sq1", [P, TG])
        u_hi = sb("u_hi", [P, 2, KH, TG], F16)
        u_lo = sb("u_lo", [P, 2, KH, TG], F16)
        po = sb("po", [P, 2, TILES, WO])
        s_sum = sb("s_sum", [P, TILES])
        s_mean = sb("s_mean", [P, TILES])
        s_msq = sb("s_msq", [P, TILES])
        s_var = sb("s_var", [P, TILES])
        s_rs = sb("s_rs", [P, TILES])
        s_alpha = sb("s_alpha", [P, TILES])
        s_beta = sb("s_beta", [P, TILES])
        w1_f, w2_f = [u_lo[:, g, :, :].rearrange("p a b -> p (a b)").bitcast(F32).rearrange("p (k n) -> p k n", k=k)
                      for g, k in ((0, KD), (1, KH))]
        scratch = gf[:, 0:4, :].rearrange("p a b -> p (a b)")
        wide = sq[:, 0:2, :].rearrange("p a b -> p (a b)").rearrange("p (k n) -> p k n", k=KH)
        wide2 = sq[:, 2:4, :].rearrange("p a b -> p (a b)").rearrange("p (k n) -> p k n", k=KH)

        T = [ps("T0"), ps("T1")]
        H = [ps("H0"), ps("H1")]
        O = [ps("O0"), ps("O1")]
        X = [ps("X0"), ps("X1")]
        SQ_PS = O[0][:, 300:300 + TILES]

        small_in = sem("small_in")
        w_in = sem("w_in")
        idx_in = [sem(f"idx_in{c}") for c in range(CHUNKS)]
        gathered = [sem(f"gathered{c}") for c in range(CHUNKS)]
        stored = [sem(f"stored{c}") for c in range(CHUNKS)]
        pool_const = sem("pool_const")
        prep_v = sem("prep_v")
        prep_a = sem("prep_a")
        abs_ps = sem("abs_ps")
        bias_ps = sem("bias_ps")
        h_ready = sem("h_ready")
        st1_done = sem("st1_done")
        mv1_done = sem("mv1_done")
        rs1_sum = sem("rs1_sum")
        nm1_done = sem("nm1_done")
        rs1_done = sem("rs1_done")
        nb1_done = sem("nb1_done")
        xn_done = sem("xn_done")
        xt_ps = sem("xt_ps")
        xt_done = sem("xt_done")
        proj_ps = sem("proj_ps")
        xb_done = sem("xb_done")
        bt_done = sem("bt_done")
        xa_done = sem("xa_done")
        delta_done = sem("delta_done")
        carry_done = sem("carry_done")
        dsum_done = sem("dsum_done")
        dA_done = sem("dA_done")
        ct_done = sem("ct_done")
        lc_done = sem("lc_done")
        r0_done = sem("r0_done")
        ct2_done = sem("ct2_done")
        er_done = sem("er_done")
        rn_done = sem("rn_done")
        v_done = sem("v_done")
        z_done = sem("z_done")
        ssum_done = sem("ssum_done")
        g_done = sem("g_done")
        y_ps = sem("y_ps")
        h2_done = sem("h2_done")
        st2_done = sem("st2_done")
        mv2_done = sem("mv2_done")
        rs2_sum = sem("rs2_sum")
        rs2_done = sem("rs2_done")
        xn2_done = sem("xn2_done")
        end_added = sem("end_added")
        x2_ps = sem("x2_ps")
        x_hi_done = sem("x_hi_done")
        x_lo_done = sem("x_lo_done")
        hid_ps = sem("hid_ps")
        gelu_done = sem("gelu_done")
        sq_done = sem("sq_done")
        u_hi_done = sem("u_hi_done")
        u_done = sem("u_done")
        sq_sum = sem("sq_sum")
        o_ps = sem("o_ps")
        po_done = sem("po_done")
        sq_ps = sem("sq_ps")
        tiny = sem("tiny")
        s_rs_done = sem("s_rs_done")
        fin_q = sem("fin_q")
        out_done = sem("out_done")

        held_v, held_p = sem("held_v"), sem("held_p")

        small = [(a_col, a_log), (bb_col, b_bias), (bd_col, d_bias), (g1_col, ln1_g), (b1n_col, ln1_b),
                 (b1_col, b1), (g2_col, ln2_g), (b2n_col, ln2_b), (wo2, wo_t)]
        rows = [(tok_bias_b, tok_bias), (bo_b, bo), (b2_b, b2)]
        SMALL = 16 * (len(small) + len(rows) + 1)

        block = ctx.enter_context(nc.Block())

        @block.sync
        def _(sp):
            def load_idx(v):
                if not zero(v.pair):
                    sp.wait_ge(gathered[v.slot], v.pair * (16 * UT))
                sp.dma_start(idx[:, v.slot, :], tokens[bass.ds(v.pair * CHUNKS + v.slot, 1), :, :].rearrange(
                    "a p t -> (a p) t")).then_inc(idx_in[v.slot], 16)

            def store(v, g):
                sp.wait_ge(out_done, v.n * UT + (g + 1) * TILES)
                dst = out[bass.ds(v.pair * 2 + g, 1), v.slot * TG:(v.slot + 1) * TG, :].rearrange(
                    "a (t p) d -> p (a t) d", p=P)
                sp.dma_start(dst, E[:, v.slot, g * TILES:(g + 1) * TILES, :]).then_inc(stored[v.slot], 16)

            for c in range(CHUNKS - 1):
                load_idx(Unit(0, c))
            sp.dma_start(w1_f[:, :, :], w1_t.rearrange("(k p) n -> p k n", p=P)).then_inc(w_in, 16)
            sp.dma_start(w2_f[:, :, :], w2_t.rearrange("(k p) n -> p k n", p=P)).then_inc(w_in, 16)
            for dst, src in rows:
                sp.dma_start(dst[:, :], src.partition_broadcast(P)).then_inc(small_in, 16)
            for dst, src in small:
                sp.dma_start(dst[:, :], src).then_inc(small_in, 16)
            sp.dma_start(proj[:, :, :], proj_w.rearrange("(k p) n -> p k n", p=P)).then_inc(small_in, 16)

            def stage(pair, k, left):
                if left >= 3:
                    load_idx(Unit(pair, k + 3))
                if k or not zero(pair):
                    store(Unit(pair, k - 1), 1)
                store(Unit(pair, k), 0)

            schedule(sp, stage)
            store(Unit(PAIRS - 1, CHUNKS - 1), 1)
            for c in range(CHUNKS):
                sp.wait_ge(stored[c], 32 * PAIRS)

        @block.gpsimd
        def _(pool):
            nc.gpsimd.memset(ones[:, :], 1.0).then_inc(pool_const, 1)
            nc.gpsimd.memset(ones_row[:, :], 1.0).then_inc(pool_const, 1)
            nc.gpsimd.memset(half[:, :], -0.5).then_inc(pool_const, 1)
            pool.wait_ge(pool_const, 3)
            nc.gpsimd.affine_select(out=ident[:, :], in_=ones[:, :], pattern=[[-1, P]], compare_op=ALU.is_equal,
                                    fill=0.0, base=0, channel_multiplier=1).then_inc(pool_const, 1)

            def gather(v):
                pool.wait_ge(idx_in[v.slot], (v.pair + 1) * 16)
                if not zero(v.pair):
                    pool.wait_ge(stored[v.slot], v.pair * 32)
                pool.sem_inc(held_p, 1)
                for t in range(UT):
                    nc.gpsimd.indirect_dma_start(
                        out=E[:, v.slot, t, :], out_offset=None, in_=table,
                        in_offset=bass.IndirectOffsetOnAxis(ap=idx[:, v.slot, t:t + 1], axis=0),
                    ).then_inc(gathered[v.slot], 16)

            def add_row(v, row):
                return nc.gpsimd.tensor_tensor(E[:, v.slot, :, :], E[:, v.slot, :, :],
                                               row[:, :].unsqueeze(1).broadcast_to([P, UT, D]), ALU.add)

            def embed(v):
                pool.wait_ge(gathered[v.slot], (v.pair + 1) * (16 * UT))
                add_row(v, tok_bias_b).then_inc(h_ready, 1)

            def norm1(v):
                if not zero(v.n):
                    pool.wait_ge(xn_done, v.n * 2)
                pool.wait_ge(mv1_done, v.n + 1)
                pool.sem_inc(held_p, 1)
                nc.gpsimd.tensor_scalar(rs1[:, :], mv1[:, :, 1], 1.0, LN_EPS, ALU.mult, ALU.add).then_inc(rs1_sum, 1)
                pool.wait_ge(rs1_sum, v.n + 1)
                nc.gpsimd.tensor_tensor(rs1[:, :], rs1[:, :], half[:, :], ALU.pow).then_inc(rs1_done, 1)
                pool.wait_ge(nm1_done, v.n + 1)
                pool.wait_ge(rs1_done, v.n + 1)
                nc.gpsimd.tensor_tensor(nb1[:, :], nm1[:, :], rs1[:, :], ALU.mult).then_inc(nb1_done, 1)

            def norm2(v):
                pool.wait_ge(mv2_done, v.n + 1)
                pool.sem_inc(held_p, 1)
                nc.gpsimd.tensor_scalar(rs2[:, :], mv2[:, :, 1], 1.0 + LN_EPS, LN_EPS * LN_EPS, ALU.mult,
                                        ALU.add).then_inc(rs2_sum, 1)
                pool.wait_ge(rs2_sum, v.n + 1)
                nc.gpsimd.tensor_tensor(rs2[:, :], rs2[:, :], half[:, :], ALU.pow).then_inc(rs2_done, 1)

            def add_end(v):
                pool.wait_ge(xn2_done, v.n * 2 + 2)
                add_row(v, end_bias_b).then_inc(end_added, 1)

            def sum_squares(n):
                pool.wait_ge(sq_done, n * 4 + 4)
                nc.gpsimd.tensor_tensor(sq4[:, :, :], sq[:, 0:4, :], sq[:, 4:8, :], ALU.add).then_inc(sq_sum, 1)
                pool.wait_ge(sq_sum, n * 3 + 1)
                nc.gpsimd.tensor_tensor(sq4[:, 0:2, :], sq4[:, 0:2, :], sq4[:, 2:4, :], ALU.add).then_inc(sq_sum, 1)
                pool.wait_ge(sq_sum, n * 3 + 2)
                if not zero(n):
                    pool.wait_ge(sq_ps, n)
                nc.gpsimd.tensor_tensor(sq1[:, :], sq4[:, 0, :], sq4[:, 1, :], ALU.add).then_inc(sq_sum, 1)

            def root_hidden(n):
                pool.wait_ge(tiny, n * TINY + 5)
                nc.gpsimd.tensor_tensor(s_rs[:, :], s_var[:, :], half[:, 0:TILES], ALU.pow).then_inc(s_rs_done, 1)

            for c in range(3):
                gather(Unit(0, c))
            pool.wait_ge(pool_const, 4)
            pool.wait_ge(small_in, SMALL)
            embed(Unit(0, 0))
            norm1(Unit(0, 0))
            embed(Unit(0, 1))
            norm1(Unit(0, 1))
            norm2(Unit(0, 0))
            add_end(Unit(0, 0))

            def stage(pair, k, left):
                n = Unit(pair, k).n
                if left >= 2:
                    embed(Unit(pair, k + 2))
                if not zero(n):
                    root_hidden(n * 2 - 1)
                if left >= 2:
                    norm1(Unit(pair, k + 2))
                sum_squares(n * 2)
                if left >= 3:
                    gather(Unit(pair, k + 3))
                root_hidden(n * 2)
                if left >= 1:
                    norm2(Unit(pair, k + 1))
                sum_squares(n * 2 + 1)
                if left >= 1:
                    add_end(Unit(pair, k + 1))

            schedule(pool, stage)
            root_hidden(UNITS * 2 - 1)

        @block.scalar
        def _(act):
            def normalise1(v, h):
                act.wait_ge(nb1_done, v.n + 1)
                if not zero(v.n):
                    act.wait_ge(xt_ps, v.n * 2)
                for t in range(h * TILES, (h + 1) * TILES):
                    last = nc.scalar.activation(xn[:, t, :], E[:, v.slot, t, :], ACT.Identity, scale=rs1[:, t:t + 1],
                                                bias=nb1[:, t:t + 1])
                    if t % TILES == TILES - 1:
                        last.then_inc(xn_done, 1)

            def copy_xt(v, h):
                act.wait_ge(xt_ps, v.n * 2 + (h + 1))
                if not zero(v.n):
                    act.wait_ge(proj_ps, v.n)
                nc.scalar.copy(xnT[:, 0, h, :], T[0][:, :])
                nc.scalar.copy(xnT[:, 1, h, :], T[1][:, :]).then_inc(xt_done, 1)

            def projected(v):
                act.wait_ge(proj_ps, v.n + 1)
                if not zero(v.n):
                    act.wait_ge(delta_done, v.n)
                nc.scalar.activation(xb[0:N, :], X[0][N:P, :], ACT.Identity, bias=bd_col[N:P, :]).then_inc(xb_done, 1)
                nc.scalar.activation(xb[N:P, :], X[1][0:N, :], ACT.Identity, bias=bd_col[0:N, :]).then_inc(xb_done, 1)
                if not zero(v.n):
                    act.wait_ge(z_done, v.n)
                nc.scalar.activation(bt[0:N, :], X[0][0:N, :], ACT.Identity, bias=bb_col[0:N, :]).then_inc(bt_done, 1)
                nc.scalar.activation(bt[N:P, :], X[1][N:P, :], ACT.Identity, bias=bb_col[N:P, :]).then_inc(bt_done, 1)

            def softplus_part(v):
                act.wait_ge(xb_done, v.n * 2 + 2)
                nc.scalar.activation(xa[:, :], xb[:, :], ACT.Abs).then_inc(xa_done, 1)
                act.wait_ge(xa_done, v.n * 3 + 1)
                nc.scalar.activation(xa[:, :], xa[:, :], ACT.Exp, scale=-1.0).then_inc(xa_done, 1)
                act.wait_ge(xa_done, v.n * 3 + 2)
                nc.scalar.activation(xa[:, :], xa[:, :], ACT.Ln, bias=1.0).then_inc(xa_done, 1)

            def decay_part(v):
                act.wait_ge(delta_done, v.n + 1)
                if not zero(v.n):
                    act.wait_ge(v_done, v.n)
                nc.scalar.activation(dA[:, :], delta[:, :], ACT.Exp, scale=a_neg[:, :]).then_inc(dA_done, 1)
                act.wait_ge(dsum_done, v.n + 1)
                if not zero(v.n):
                    act.wait_ge(er_done, v.n)
                nc.scalar.activation(ct[:, :], dsum[:, v.slot % 2, 0:TG], ACT.Exp, scale=a_neg[:, :]).then_inc(ct_done, 1)
                act.wait_ge(ct_done, v.n + 1)
                nc.scalar.activation(lc[:, :], ct[:, :], ACT.Ln, bias=eps_col[:, :]).then_inc(lc_done, 1)
                act.wait_ge(lc_done, v.n + 1)
                if not zero(v.n):
                    act.wait_ge(rn_done, v.n)
                nc.scalar.activation(r0[:, :], lc[:, :], ACT.Exp, scale=-1.0).then_inc(r0_done, 1)
                if not zero(v.n):
                    act.wait_ge(g_done, v.n)
                nc.scalar.activation(ct2[:, :], ct[:, :], ACT.Square).then_inc(ct2_done, 1)

            def high_x(v, g):
                n = v.n * 2 + g
                act.wait_ge(x2_ps, n + 1)
                if not zero(v.n):
                    act.wait_ge(hid_ps, (n - 1) * KH)
                for k in range(KD):
                    nc.scalar.activation(x_hi[:, g, k, :], T[k][:, :], ACT.Identity,
                                         scale=g1_s[:, k:k + 1]).then_inc(x_hi_done, 1)

            def gelu(v, g, between={}):
                n = v.n * 2 + g

                def square(m):
                    act.wait_ge(gelu_done, n * KH + (m + 2))
                    nc.scalar.activation(sq[:, m:m + 2, :], gf[:, m:m + 2, :], ACT.Square).then_inc(sq_done, 1)

                for m in range(KH):
                    act.wait_ge(hid_ps, n * KH + (m + 1))
                    if not zero(n):
                        act.wait_ge(u_done, n * KH + (m + 1 - KH))
                        if m % 2 == 0:
                            act.wait_ge(sq_done, n * 4 + (m // 2 - 3))
                    nc.scalar.activation(gf[:, m, :], H[m % 2][:, :], ACT.Gelu, scale=gelu_scale[:, :],
                                         bias=b1_eff[:, m:m + 1]).then_inc(gelu_done, 1)
                    if m == 1 and not zero(n):
                        act.wait_ge(sq_sum, n * 3 - 2)
                    if m % 2 == 0 and m:
                        square(m - 2)
                    if m in between:
                        between[m]()
                square(KH - 2)

            def copy_out(v, g, t):
                n = v.n * 2 + g
                act.wait_ge(o_ps, n * TILES + (t + 1))
                if t == 0 and not zero(v.n):
                    act.wait_ge(out_done, (n - 1) * TILES)
                nc.scalar.copy(po[:, g, t, :], O[t % 2][:, 0:WO]).then_inc(po_done, 1)

            nc.scalar.preload_act_table_set("natural_log_exp_and_others")
            act.wait_ge(small_in, SMALL)
            nc.scalar.activation(a_soft[:, :], a_col[:, :], ACT.Abs).then_inc(prep_a, 1)
            act.wait_ge(prep_a, 1)
            nc.scalar.activation(a_soft[:, :], a_soft[:, :], ACT.Exp, scale=-1.0).then_inc(prep_a, 1)
            act.wait_ge(prep_a, 2)
            nc.scalar.activation(a_soft[:, :], a_soft[:, :], ACT.Ln, bias=1.0).then_inc(prep_a, 1)
            def embeddings_to_projections(v):
                return [lambda: normalise1(v, 0), lambda: normalise1(v, 1), lambda: copy_xt(v, 0),
                        lambda: copy_xt(v, 1), lambda: projected(v)]

            first, second = Unit(0, 0), Unit(0, 1)
            for f in embeddings_to_projections(first):
                f()
            softplus_part(first)
            decay_part(first)
            for f in embeddings_to_projections(second):
                f()
            high_x(first, 0)

            def stage(pair, k, left):
                u, after, then = Unit(pair, k), Unit(pair, k + 1), Unit(pair, k + 2)
                before = Unit(pair, k - 1)
                gelu(u, 0, {} if zero(u.n) else {0: lambda: copy_out(before, 1, 2), 1: lambda: copy_out(before, 1, 3)})
                if left >= 1:
                    nc.scalar.preload_act_table_set("natural_log_exp_and_others")
                    softplus_part(after)
                high_x(u, 1)
                copy_out(u, 0, 0)
                if left >= 1:
                    decay_part(after)
                copy_out(u, 0, 1)
                early = {0: lambda: copy_out(u, 0, 2), 1: lambda: copy_out(u, 0, 3)}
                if left >= 2:
                    early.update(zip((2, 3, 4, 5, 7), embeddings_to_projections(then)))
                gelu(u, 1, early)
                if left >= 1:
                    high_x(after, 0)
                copy_out(u, 1, 0)
                copy_out(u, 1, 1)

            schedule(act, stage)
            copy_out(Unit(PAIRS - 1, CHUNKS - 1), 1, 2)
            copy_out(Unit(PAIRS - 1, CHUNKS - 1), 1, 3)

        @block.vector
        def _(dve):
            steps = [0]

            def link(ins):
                steps[0] += 1
                ins.then_inc(prep_v, 1)
                dve.wait_ge(prep_v, steps[0])

            dve.wait_ge(w_in, 32)
            link(nc.vector.memset(eps_col[:, :], EPS))
            link(nc.vector.tensor_reduce(absum[:, 0:1], w1_f[:, :, :], AX.XY, ALU.add, apply_absolute_value=True))
            link(nc.vector.tensor_reduce(absum[:, 1:2], w2_f[:, :, :], AX.XY, ALU.add, apply_absolute_value=True))
            assert steps[0] == ABSUM_STEPS
            dve.wait_ge(abs_ps, 1)
            link(nc.vector.tensor_scalar(wscale[:, :], X[0][:, 0:2], 1.0 / (D * HID), 1e-5, ALU.mult, ALU.max))
            link(nc.vector.reciprocal(winv[:, :], wscale[:, :]))
            link(nc.vector.tensor_scalar(gelu_scale[:, :], wscale[:, 0:1], 1.0 / XS, None, ALU.mult))
            link(nc.vector.tensor_scalar(alpha_scale[:, :], wscale[:, 1:2], 1.0 / US, None, ALU.mult))
            for i, (w, c) in enumerate(((w1_f, KD), (w2_f, KH))):
                flat = w.rearrange("p a b -> p (a b)")
                link(nc.vector.tensor_scalar(scratch, flat, winv[:, i:i + 1], 0.5, ALU.mult, ALU.is_gt))
                link(nc.vector.tensor_scalar(flat, flat, winv[:, i:i + 1], -0.5, ALU.mult, ALU.is_lt))
                link(nc.vector.tensor_tensor(flat, scratch, flat, ALU.subtract))
            link(nc.vector.tensor_copy(t1[:, :, :], w1_f[:, :, :]))
            dve.wait_ge(small_in, SMALL)
            link(nc.vector.tensor_scalar(g2_zero[:, :], g2_col[:, :], 0.0, None, ALU.is_equal))
            link(nc.vector.tensor_scalar(g2_some[:, :], g2_zero[:, :], -1.0, 1.0, ALU.mult, ALU.add))
            link(nc.vector.tensor_tensor(g2_safe[:, :], g2_col[:, :], g2_zero[:, :], ALU.add))
            link(nc.vector.tensor_scalar(g2_s[:, :], g2_safe[:, :], US, None, ALU.mult))
            link(nc.vector.reciprocal(g2_inv[:, :], g2_safe[:, :]))
            for k in range(KH):
                link(nc.vector.tensor_scalar(t2[:, k, 0:D], w2_f[:, k, :], g2_some[:, k:k + 1], None, ALU.mult))
            link(nc.vector.tensor_copy(t2[:, :, D], g2_inv[:, :]))
            link(nc.vector.tensor_tensor(t2[:, :, D + 1], g2_inv[:, :], t2[:, :, D], ALU.subtract))
            link(nc.vector.tensor_copy(wide, g2_col[:, :].unsqueeze(2).broadcast_to([P, KH, P])))
            link(nc.vector.tensor_copy(wide2, b2n_col[:, :].unsqueeze(2).broadcast_to([P, KH, P])))
            assert steps[0] == WIDE_STEPS
            link(nc.vector.tensor_scalar(g1_s[:, :], g1_col[:, :], XS, None, ALU.mult))
            dve.wait_ge(prep_a, 3)
            link(nc.vector.scalar_tensor_tensor(a_neg[:, :], a_col[:, :], 0.0, a_soft[:, :], ALU.max, ALU.add))
            link(nc.vector.tensor_scalar(a_neg[:, :], a_neg[:, :], -1.0, None, ALU.mult))
            link(nc.vector.tensor_scalar(a_inv[:, :], a_neg[:, :], EPS, -1.0, ALU.add, ALU.mult))
            link(nc.vector.reciprocal(a_inv[:, :], a_inv[:, :]))
            dve.wait_ge(bias_ps, 1)
            link(nc.vector.scalar_tensor_tensor(b1_eff[:, :], T[0][:, 0:KH], wscale[:, 0:1], b1_col[:, :], ALU.mult,
                                                ALU.add))
            link(nc.vector.tensor_copy(colsum_b[:, :], X[0][:, 0:D]))
            link(nc.vector.scalar_tensor_tensor(end_bias_b[:, :], X[1][:, 0:D], wscale[:, 1:2], b2_b[:, :], ALU.mult,
                                                ALU.add))
            link(nc.vector.memset(ones_bf[:, :], 1.0))
            link(nc.vector.memset(bo_parts[:, :, :], 0.0))
            for q in (0, 32, 64):
                row = bo_parts[q:q + 1, 0, :]
                link(nc.vector.tensor_copy(row, bo_b[q:q + 1, :] if q == 0 else bo_rest[q:q + 1, :]))
                link(nc.vector.tensor_copy(bo_parts[q:q + 1, 1, :], row))
                if q == 0:
                    link(nc.vector.tensor_copy(bo_hi[:, :], bo_b[:, :]))
                    link(nc.vector.tensor_tensor(bo_rest[:, :], bo_b[:, :], bo_hi[:, :], ALU.subtract))
                if q == 32:
                    link(nc.vector.tensor_copy(bo_hi[:, :], bo_rest[:, :]))
                    link(nc.vector.tensor_tensor(bo_rest[:, :], bo_rest[:, :], bo_hi[:, :], ALU.subtract))
            assert steps[0] == PREP_STEPS
            dve.wait_ge(pool_const, 4)

            def stats(v, st, mv, st_done, mv_done):
                for t in range(UT):
                    last = nc.vector.bn_stats(st[:, t, :], E[:, v.slot, t, :])
                last.then_inc(st_done, 1)
                dve.wait_ge(st_done, v.n + 1)
                dve.sem_inc(held_v, 1)
                for t in range(UT):
                    last = nc.vector.bn_aggr(mv[:, t, :], st[:, t, :])
                last.then_inc(mv_done, 1)

            def normalise(v, dst, mv, rs, done):
                for t in range(UT):
                    last = nc.vector.tensor_scalar(dst[:, t, :], E[:, v.slot, t, :], mv[:, t, 0:1], rs[:, t:t + 1],
                                                   ALU.subtract, ALU.mult)
                    if t % TILES == TILES - 1:
                        last.then_inc(done, 1)

            def stats1(v):
                dve.wait_ge(h_ready, v.n + 1)
                if not zero(v.n):
                    dve.wait_ge(nb1_done, v.n)
                stats(v, st1, mv1, st1_done, mv1_done)
                dve.wait_ge(mv1_done, v.n + 1)
                nc.vector.tensor_scalar(nm1[:, :], mv1[:, :, 0], -1.0, None, ALU.mult).then_inc(nm1_done, 1)

            def step_sums(v):
                b = v.slot % 2
                dve.wait_ge(xa_done, v.n * 3 + 3)
                if not zero(v.n):
                    dve.wait_ge(dA_done, v.n)
                nc.vector.scalar_tensor_tensor(delta[:, :], xb[:, :], 0.0, xa[:, :], ALU.max, ALU.add).then_inc(delta_done, 1)
                if not zero(v.n):
                    dve.wait_ge(ct_done, v.n)
                if v.slot == 0:
                    nc.vector.memset(dsum[:, b, 0:1], 0.0).then_inc(carry_done, 1)
                else:
                    dve.wait_ge(dsum_done, v.n)
                    nc.vector.tensor_copy(dsum[:, b, 0:1], dsum[:, 1 - b, TG:TG + 1]).then_inc(carry_done, 1)
                dve.wait_ge(delta_done, v.n + 1)
                dve.wait_ge(carry_done, v.n + 1)
                nc.vector.tensor_tensor_scan(dsum[:, b, 1:TG + 1], ones_row[:, :], delta[:, :], dsum[:, b, 0:1],
                                             ALU.mult, ALU.add).then_inc(dsum_done, 1)

            def recurrence(v):
                b = v.slot % 2
                dve.wait_ge(r0_done, v.n + 1)
                nc.vector.scalar_tensor_tensor(er[:, :], ct[:, :], EPS, r0[:, :], ALU.add, ALU.mult).then_inc(er_done, 1)
                dve.wait_ge(er_done, v.n + 1)
                nc.vector.scalar_tensor_tensor(rn[:, :], er[:, :], -2.0, r0[:, :], ALU.add, ALU.mult).then_inc(rn_done, 1)
                dve.wait_ge(rn_done, v.n + 1)
                dve.wait_ge(dA_done, v.n + 1)
                nc.vector.scalar_tensor_tensor(zz[:, :], dA[:, :], -1.0, rn[:, :], ALU.add, ALU.mult).then_inc(v_done, 1)
                dve.wait_ge(v_done, v.n + 1)
                dve.wait_ge(bt_done, v.n * 2 + 2)
                nc.vector.tensor_tensor(zz[:, :], bt[:, :], zz[:, :], ALU.mult).then_inc(z_done, 1)
                dve.wait_ge(z_done, v.n + 1)
                if v.slot:
                    dve.wait_ge(ssum_done, v.n)
                nc.vector.tensor_tensor_scan(ssum[:, b, :], ones_row[:, :], zz[:, :],
                                             ssum[:, 1 - b, TG - 1:TG] if v.slot else 0.0,
                                             ALU.mult, ALU.add).then_inc(ssum_done, 1)
                dve.wait_ge(ssum_done, v.n + 1)
                dve.wait_ge(ct2_done, v.n + 1)
                if not zero(v.n):
                    dve.wait_ge(y_ps, v.n * 4)
                nc.vector.scalar_tensor_tensor(G[:, :], ssum[:, b, :], a_inv[:, :], ct2[:, :], ALU.mult,
                                               ALU.mult).then_inc(g_done, 1)

            def residual(v, q):
                dve.wait_ge(y_ps, v.n * 4 + (q + 1))
                e = E[:, v.slot, 2 * q:2 * q + 2, :].rearrange("p t d -> p (t d)")
                nc.vector.tensor_tensor(e, X[q % 2][:, :], e, ALU.add).then_inc(h2_done, 1)

            def stats2(v):
                dve.wait_ge(h2_done, v.n * 4 + 4)
                stats(v, st2, mv2, st2_done, mv2_done)

            def normalise2(v):
                dve.wait_ge(rs2_done, v.n + 1)
                if not zero(v.n):
                    dve.wait_ge(x2_ps, v.n * 2)
                normalise(v, xn2, mv2, rs2, xn2_done)

            def low_x(v, g):
                n = v.n * 2 + g
                if not zero(v.n):
                    dve.wait_ge(hid_ps, (n - 1) * KH)
                for k in range(KD):
                    dve.wait_ge(x_hi_done, n * 2 + (k + 1))
                    nc.vector.scalar_tensor_tensor(x_lo[:, g, k, :], T[k][:, :], g1_s[:, k:k + 1], x_hi[:, g, k, :],
                                                   ALU.mult, ALU.subtract).then_inc(x_lo_done, 1)

            def step(n, i, ins):
                ins.then_inc(tiny, 1)
                dve.wait_ge(tiny, n * TINY + i)

            def hidden_variance(n, g):
                dve.wait_ge(po_done, n * TILES + TILES)
                step(n, 1, nc.vector.tensor_tensor(s_sum[:, :], po[:, g, :, D], po[:, g, :, D + 1], ALU.add))
                step(n, 2, nc.vector.tensor_scalar(s_mean[:, :], s_sum[:, :], 1.0 / (US * HID), None, ALU.mult))
                step(n, 3, nc.vector.tensor_tensor(s_msq[:, :], s_mean[:, :], s_mean[:, :], ALU.mult))
                dve.wait_ge(sq_ps, n + 1)
                step(n, 4, nc.vector.scalar_tensor_tensor(s_var[:, :], SQ_PS, 1.0 / HID, s_msq[:, :], ALU.mult,
                                                          ALU.subtract))
                step(n, 5, nc.vector.tensor_scalar(s_var[:, :], s_var[:, :], 0.0, LN_EPS, ALU.max, ALU.add))

            def hidden_scales(n):
                dve.wait_ge(s_rs_done, n + 1)
                step(n, 6, nc.vector.tensor_scalar(s_alpha[:, :], s_rs[:, :], alpha_scale[:, :], None, ALU.mult))
                step(n, 7, nc.vector.scalar_tensor_tensor(s_beta[:, :], s_mean[:, :], -US, s_alpha[:, :], ALU.mult,
                                                          ALU.mult))

            def finish_first(v, g, t):
                n = v.n * 2 + g
                if t == 0:
                    dve.wait_ge(tiny, n * TINY + 7)
                    dve.wait_ge(end_added, v.n + 1)
                nc.vector.scalar_tensor_tensor(E[:, v.slot, g * TILES + t, :], colsum_b[:, :], s_beta[:, t:t + 1],
                                               E[:, v.slot, g * TILES + t, :], ALU.mult, ALU.add).then_inc(fin_q, 1)

            def finish_last(v, g, t):
                n = v.n * 2 + g
                dve.wait_ge(fin_q, n * TILES + (t + 1))
                nc.vector.scalar_tensor_tensor(E[:, v.slot, g * TILES + t, :], po[:, g, t, 0:D], s_alpha[:, t:t + 1],
                                               E[:, v.slot, g * TILES + t, :], ALU.mult, ALU.add).then_inc(out_done, 1)

            def finish(v, g):
                for t in range(TILES):
                    finish_first(v, g, t)
                for t in range(TILES):
                    finish_last(v, g, t)

            def split_hidden(v, g, between={}):
                n = v.n * 2 + g
                if not zero(v.n):
                    dve.wait_ge(o_ps, (n - 1) * TILES)

                def high(m):
                    dve.wait_ge(gelu_done, n * KH + (m + 1))
                    nc.vector.tensor_scalar(u_hi[:, g, m, :], gf[:, m, :], g2_s[:, m:m + 1], None,
                                            ALU.mult).then_inc(u_hi_done, 1)

                high(0)
                for m in range(KH):
                    if m + 1 < KH:
                        high(m + 1)
                    dve.wait_ge(u_hi_done, n * KH + (m + 1))
                    nc.vector.scalar_tensor_tensor(u_lo[:, g, m, :], gf[:, m, :], g2_s[:, m:m + 1], u_hi[:, g, m, :],
                                                   ALU.mult, ALU.subtract).then_inc(u_done, 1)
                    for f in between.get(m, ()):
                        f()

            first = Unit(0, 0)
            stats1(first)
            step_sums(first)
            recurrence(first)
            stats1(Unit(0, 1))
            for q in range(4):
                residual(first, q)
            stats2(first)
            normalise2(first)
            low_x(first, 0)

            def stage(pair, k, left):
                u, after, then = Unit(pair, k), Unit(pair, k + 1), Unit(pair, k + 2)
                before, n = Unit(pair, k - 1), u.n * 2
                split_hidden(u, 0, {
                    2: [] if zero(u.n) else [lambda: hidden_variance(n - 1, 1)],
                    4: [] if zero(u.n) else [lambda: hidden_scales(n - 1)],
                    5: [lambda: stats1(then)] if left >= 2 else []})
                low_x(u, 1)
                if left >= 1:
                    step_sums(after)
                if not zero(u.n):
                    finish(before, 1)
                if left >= 1:
                    recurrence(after)
                    residual(after, 0)
                    residual(after, 1)
                split_hidden(u, 1, {
                    2: [lambda: hidden_variance(n, 0)],
                    3: [lambda: residual(after, 2), lambda: residual(after, 3)] if left >= 1 else [],
                    4: [lambda: stats2(after)] if left >= 1 else [],
                    5: [lambda: hidden_scales(n)],
                    6: [lambda: normalise2(after)] if left >= 1 else []})
                if left >= 1:
                    low_x(after, 0)
                finish(u, 0)

            schedule(dve, stage)
            last, n = Unit(PAIRS - 1, CHUNKS - 1), UNITS * 2 - 1
            hidden_variance(n, 1)
            hidden_scales(n)
            finish(last, 1)

        @block.tensor
        def _(pe):
            pe.wait_ge(pool_const, 4)
            pe.wait_ge(prep_v, ABSUM_STEPS)
            nc.tensor.matmul(X[0][:, 0:2], ones[:, :], absum[:, :], start=True, stop=True).then_inc(abs_ps, 1)
            pe.wait_ge(prep_v, WIDE_STEPS)
            for m in range(KH):
                for k in range(KD):
                    nc.tensor.matmul(T[0][:, m:m + 1], w1_f[:, k, m * P:(m + 1) * P], b1n_col[:, k:k + 1],
                                     start=(k == 0), stop=(k == KD - 1))
            for w, x in ((wide, X[0]), (wide2, X[1])):
                for k in range(KH):
                    last = nc.tensor.matmul(x[:, 0:D], w[:, k, :], w2_f[:, k, :], start=(k == 0), stop=(k == KH - 1))
            last.then_inc(bias_ps, 1)
            pe.wait_ge(prep_v, PREP_STEPS)

            def turn(x, g, done):
                for k in range(KD):
                    for t in range(TILES):
                        last = nc.tensor.transpose(T[k][:, t * P:(t + 1) * P], x[:, g * TILES + t, k * P:(k + 1) * P],
                                                   ident[:, :])
                last.then_inc(done, 1)

            def turn_embeddings(v, h):
                pe.wait_ge(xn_done, v.n * 2 + (h + 1))
                turn(xn, h, xt_ps)

            def project(v):
                pe.wait_ge(xt_done, v.n * 2 + 2)
                if not zero(v.n):
                    pe.wait_ge(h2_done, v.n * 4)
                for h in range(2):
                    for k in range(KD):
                        last = nc.tensor.matmul(X[h][:, :], proj[:, k, h * P:(h + 1) * P], xnT[:, k, h, :],
                                                start=(k == 0), stop=(k == KD - 1))
                last.then_inc(proj_ps, 1)

            def attention_out(v, q):
                h = q // 2
                pe.wait_ge(g_done, v.n + 1)
                pe.wait_ge(bt_done, v.n * 2 + 2)
                if q >= 2 or not zero(v.n):
                    pe.wait_ge(h2_done, v.n * 4 + (q - 1 if q >= 2 else 0))
                nc.tensor.matmul(X[q % 2][:, :], ones_bf[:, :], bo_parts[:, :, :], start=True, stop=False)
                for i in range(2):
                    t = (q % 2) * 2 + i
                    last = nc.tensor.matmul(X[q % 2][:, i * D:(i + 1) * D], G[h * N:(h + 1) * N, t * P:(t + 1) * P],
                                            wo2[h * N:(h + 1) * N, :], start=False, stop=(i == 1))
                last.then_inc(y_ps, 1)

            def turn_stream(v, g):
                pe.wait_ge(xn2_done, v.n * 2 + (g + 1))
                turn(xn2, g, x2_ps)

            def square_sums(n):
                pe.wait_ge(sq_sum, n * 3 + 3)
                pe.wait_ge(po_done, n * TILES + 3)
                for t in range(TILES):
                    last = nc.tensor.matmul(SQ_PS[:, t:t + 1], sq1[:, t * P:(t + 1) * P], ones[:, 0:1], start=True,
                                            stop=True)
                last.then_inc(sq_ps, 1)

            def first_product(v, g, chunks, between={}):
                n = v.n * 2 + g
                pe.wait_ge(x_hi_done, n * 2 + 2)
                pe.wait_ge(x_lo_done, n * 2 + 2)
                for m in chunks:
                    if not (zero(n) and m < 2):
                        pe.wait_ge(gelu_done, n * KH + (m - 1))
                    for k in range(KD):
                        for x in (x_hi, x_lo):
                            last = nc.tensor.matmul(H[m % 2][:, :], t1[:, k, m * P:(m + 1) * P], x[:, g, k, :],
                                                    start=(k == 0 and x is x_hi), stop=(k == KD - 1 and x is x_lo))
                    last.then_inc(hid_ps, 1)
                    for f in between.get(m, ()):
                        f()

            def second_product(v, g, tiles):
                n = v.n * 2 + g
                if tiles[0] == 0 and not zero(n):
                    pe.wait_ge(tiny, n * TINY - 3)
                for t in tiles:
                    if not (zero(n) and t < 2):
                        pe.wait_ge(po_done, n * TILES + (t - 1))
                    for k in range(KH):
                        if t == 0:
                            pe.wait_ge(u_done, n * KH + (k + 1))
                        for x in (u_hi, u_lo):
                            last = nc.tensor.matmul(O[t % 2][:, 0:WO], x[:, g, k, t * P:(t + 1) * P], t2[:, k, :],
                                                    start=(k == 0 and x is u_hi), stop=(k == KH - 1 and x is u_lo))
                    last.then_inc(o_ps, 1)

            def banks_read(xt=None, x=None):
                if xt is not None:
                    pe.wait_ge(xt_done, xt)
                else:
                    pe.wait_ge(x_hi_done, x * 2)
                    pe.wait_ge(x_lo_done, x * 2)

            first, second = Unit(0, 0), Unit(0, 1)
            turn_embeddings(first, 0)
            banks_read(xt=1)
            turn_embeddings(first, 1)
            project(first)
            for q in range(4):
                attention_out(first, q)
            turn_embeddings(second, 0)
            banks_read(xt=3)
            turn_embeddings(second, 1)
            project(second)
            turn_stream(first, 0)
            first_product(first, 0, (0, 1))

            def stage(pair, k, left):
                u, after, then = Unit(pair, k), Unit(pair, k + 1), Unit(pair, k + 2)
                n = u.n * 2
                first_product(u, 0, range(2, KH), {2: [] if zero(u.n) else [lambda: square_sums(n - 1)]})
                banks_read(x=n + 1)
                turn_stream(u, 1)
                second_product(u, 0, (0, 1))
                first_product(u, 1, (0, 1))
                second_product(u, 0, (2, 3))
                if left >= 1:
                    attention_out(after, 0)
                    attention_out(after, 1)

                def embeddings(h):
                    if h == 0:
                        banks_read(x=n + 2)
                    else:
                        banks_read(xt=then.n * 2 + 1)
                    turn_embeddings(then, h)

                first_product(u, 1, range(2, KH), {
                    2: [lambda: square_sums(n)],
                    3: [lambda: attention_out(after, 2), lambda: attention_out(after, 3)] if left >= 1 else [],
                    4: [lambda: embeddings(0)] if left >= 2 else [],
                    5: [lambda: embeddings(1)] if left >= 2 else [],
                    6: [lambda: project(then)] if left >= 2 else []})
                if left >= 2:
                    banks_read(xt=then.n * 2 + 2)
                elif left >= 1:
                    banks_read(x=n + 2)
                if left >= 1:
                    turn_stream(after, 0)
                second_product(u, 1, (0, 1))
                if left >= 1:
                    first_product(after, 0, (0, 1))
                second_product(u, 1, (2, 3))

            schedule(pe, stage)
            square_sums(UNITS * 2 - 1)


ABSUM_STEPS = 3
WIDE_STEPS = 3 + 4 + 6 + 1 + 5 + KH + 4
PREP_STEPS = WIDE_STEPS + 1 + 4 + 3 + 12


def kernel(x, L0_tok_weight, L0_tok_bias, L0_attn_A_log, L0_attn_WB, L0_attn_bB, L0_attn_WC, L0_attn_bC, L0_attn_Wd,
           L0_attn_bd, L0_attn_Wo, L0_attn_bo, L0_ffn_ln1_g, L0_ffn_ln1_b, L0_ffn_w1, L0_ffn_b1, L0_ffn_ln2_g,
           L0_ffn_ln2_b, L0_ffn_w2, L0_ffn_b2):
    import numpy as np
    import concourse.bacc as bacc
    from concourse.bass_utils import run_bass_kernel_spmd

    def twice(a):
        return np.concatenate([a, a]).reshape(P, 1)

    def column(a):
        return np.ascontiguousarray(np.asarray(a).reshape(-1, P).T)

    wb, wd = np.asarray(L0_attn_WB).T, np.repeat(np.asarray(L0_attn_Wd).T, N, axis=1)
    wo = np.asarray(L0_attn_Wo).T
    arrays = {
        "tokens": np.ascontiguousarray(np.asarray(x).reshape(PAIRS, 2, CHUNKS, TILES, P).transpose(0, 2, 4, 1, 3)
                                       .reshape(UNITS, P, UT)),
        "table": np.ascontiguousarray(np.asarray(L0_tok_weight).T),
        "tok_bias": np.asarray(L0_tok_bias),
        "a_log": twice(np.asarray(L0_attn_A_log)),
        "b_bias": twice(np.asarray(L0_attn_bB)),
        "d_bias": np.repeat(np.asarray(L0_attn_bd), P).reshape(P, 1),
        "proj_w": np.ascontiguousarray(np.concatenate([wb, wd, wd, wb], axis=1)),
        "wo_t": np.ascontiguousarray(np.concatenate([wo, wo])),
        "bo": np.asarray(L0_attn_bo),
        "ln1_g": column(L0_ffn_ln1_g),
        "ln1_b": column(L0_ffn_ln1_b),
        "w1_t": np.ascontiguousarray(np.asarray(L0_ffn_w1).T),
        "b1": column(L0_ffn_b1),
        "ln2_g": column(L0_ffn_ln2_g),
        "ln2_b": column(L0_ffn_ln2_b),
        "w2_t": np.ascontiguousarray(np.asarray(L0_ffn_w2).T),
        "b2": np.asarray(L0_ffn_b2),
    }
    nc = bacc.Bacc("TRN2", target_bir_lowering=False, num_devices=1)
    given = {k: nc.dram_tensor(k, a.shape, mybir.dt.from_np(a.dtype), kind="ExternalInput").ap()
             for k, a in arrays.items()}
    out = nc.dram_tensor("out", (BATCH, SEQ, D), F32, kind="ExternalOutput").ap()
    lm_tower(nc, out=out, **given)
    return run_bass_kernel_spmd(nc, [arrays], core_ids=[0]).results[0]["out"]
```

```python
from contextlib import ExitStack

import concourse.bass as bass
from concourse import mybir

ALU = mybir.AluOpType
ACT = mybir.ActivationFunctionType
AX = mybir.AxisListType
F32 = mybir.dt.float32
F16 = mybir.dt.float16
BF16 = mybir.dt.bfloat16
I32 = mybir.dt.int32

P = 128
D = 256
KD = D // P
N = 64
HID = 1024
KH = HID // P
BATCH, SEQ = 8, 2048
TG = 512
TILES = TG // P
UT = 2 * TILES
CHUNKS = SEQ // TG
PAIRS = BATCH // 2
UNITS = PAIRS * CHUNKS
WO = D + 2
TINY = 7

LN_EPS = 1e-5
EPS = 1e-6
XS = 16.0
US = 32.0


class Unit:

    def __init__(self, pair, k):
        self.n = pair * CHUNKS + k
        self.slot = k % CHUNKS
        self.pair = pair + k // CHUNKS


def zero(x):
    return isinstance(x, int) and x == 0


def schedule(eng, stage):
    stage(0, 0, 9)
    with eng.Fori(0, PAIRS - 1) as pair:
        for k in range(1, CHUNKS + 1):
            stage(pair, k, 9)
    for k in range(1, CHUNKS):
        stage(PAIRS - 1, k, CHUNKS - 1 - k)


def lm_tower(nc, tokens, table, tok_bias, a_log, b_bias, d_bias, proj_w, wo_t, bo, ln1_g, ln1_b, w1_t, b1, ln2_g,
             ln2_b, w2_t, b2, out):
    with ExitStack() as ctx:
        def sb(name, shape, dt=F32):
            return ctx.enter_context(nc.sbuf_tensor(name, shape, dt))

        def ps(name):
            return ctx.enter_context(nc.psum_tensor(name, [P, TG], F32))

        def sem(name):
            return ctx.enter_context(nc.semaphore(name))

        ident = sb("ident", [P, P])
        ones = sb("ones", [P, P])
        ones_row = sb("ones_row", [P, TG])
        eps_col = sb("eps_col", [P, 1])
        half = sb("half", [P, UT])
        tok_bias_b = sb("tok_bias_b", [P, D])
        bo_b = sb("bo_b", [P, D])
        ones_bf = sb("ones_bf", [P, P], BF16)
        bo_parts = sb("bo_parts", [P, 2, D], BF16)
        bo_hi = sb("bo_hi", [P, D], BF16)
        bo_rest = sb("bo_rest", [P, D])
        b2_b = sb("b2_b", [P, D])
        end_bias_b = sb("end_bias_b", [P, D])
        colsum_b = sb("colsum_b", [P, D])
        proj = sb("proj", [P, KD, 4 * N])
        wo2 = sb("wo2", [P, D])
        t1 = sb("t1", [P, KD, HID], F16)
        t2 = sb("t2", [P, KH, WO], F16)
        absum = sb("absum", [P, 2])
        wscale = sb("wscale", [P, 2])
        winv = sb("winv", [P, 2])
        gelu_scale = sb("gelu_scale", [P, 1])
        alpha_scale = sb("alpha_scale", [P, 1])
        a_col = sb("a_col", [P, 1])
        a_soft = sb("a_soft", [P, 1])
        a_neg = sb("a_neg", [P, 1])
        a_inv = sb("a_inv", [P, 1])
        bb_col = sb("bb_col", [P, 1])
        bd_col = sb("bd_col", [P, 1])
        g1_col = sb("g1_col", [P, KD])
        g1_s = sb("g1_s", [P, KD])
        b1n_col = sb("b1n_col", [P, KD])
        b1_col = sb("b1_col", [P, KH])
        b1_eff = sb("b1_eff", [P, KH])
        g2_col = sb("g2_col", [P, KH])
        b2n_col = sb("b2n_col", [P, KH])
        g2_zero = sb("g2_zero", [P, KH])
        g2_some = sb("g2_some", [P, KH])
        g2_safe = sb("g2_safe", [P, KH])
        g2_s = sb("g2_s", [P, KH])
        g2_inv = sb("g2_inv", [P, KH])

        idx = sb("idx", [P, CHUNKS, UT], I32)
        E = sb("E", [P, CHUNKS, UT, D])
        st1 = sb("st1", [P, UT, 6])
        mv1 = sb("mv1", [P, UT, 2])
        nm1 = sb("nm1", [P, UT])
        nb1 = sb("nb1", [P, UT])
        rs1 = sb("rs1", [P, UT])
        xn = sb("xn", [P, UT, D])
        xnT = sb("xnT", [P, KD, 2, TG])
        xb = sb("xb", [P, TG])
        xa = sb("xa", [P, TG])
        bt = sb("bt", [P, TG])
        delta = sb("delta", [P, TG])
        dsum = sb("dsum", [P, 2, TG + 1])
        dA = sb("dA", [P, TG])
        ct = sb("ct", [P, TG])
        ct2 = sb("ct2", [P, TG])
        lc = sb("lc", [P, TG])
        r0 = sb("r0", [P, TG])
        er = sb("er", [P, TG])
        rn = sb("rn", [P, TG])
        zz = sb("zz", [P, TG])
        ssum = sb("ssum", [P, 2, TG])
        G = sb("G", [P, TG])
        st2 = sb("st2", [P, UT, 6])
        mv2 = sb("mv2", [P, UT, 2])
        rs2 = sb("rs2", [P, UT])
        xn2 = sb("xn2", [P, UT, D])
        x_hi = sb("x_hi", [P, 2, KD, TG], F16)
        x_lo = sb("x_lo", [P, 2, KD, TG], F16)
        gf = sb("gf", [P, KH, TG])
        sq = sb("sq", [P, KH, TG])
        sq4 = sb("sq4", [P, KH // 2, TG])
        sq1 = sb("sq1", [P, TG])
        u_hi = sb("u_hi", [P, 2, KH, TG], F16)
        u_lo = sb("u_lo", [P, 2, KH, TG], F16)
        po = sb("po", [P, 2, TILES, WO])
        s_sq = sb("s_sq", [P, TILES])
        s_sum = sb("s_sum", [P, TILES])
        s_mean = sb("s_mean", [P, TILES])
        s_msq = sb("s_msq", [P, TILES])
        s_var = sb("s_var", [P, TILES])
        s_rs = sb("s_rs", [P, TILES])
        s_alpha = sb("s_alpha", [P, TILES])
        s_beta = sb("s_beta", [P, TILES])
        w1_f, w2_f = [u_lo[:, g, :, :].rearrange("p a b -> p (a b)").bitcast(F32).rearrange("p (k n) -> p k n", k=k)
                      for g, k in ((0, KD), (1, KH))]
        scratch = gf[:, 0:4, :].rearrange("p a b -> p (a b)")
        wide = sq[:, 0:2, :].rearrange("p a b -> p (a b)").rearrange("p (k n) -> p k n", k=KH)
        wide2 = sq[:, 2:4, :].rearrange("p a b -> p (a b)").rearrange("p (k n) -> p k n", k=KH)

        T = [ps("T0"), ps("T1")]
        H = [ps("H0"), ps("H1")]
        O = [ps("O0"), ps("O1")]
        X = [ps("X0"), ps("X1")]
        SQ_PS = O[0][:, 300:300 + TILES]

        small_in = sem("small_in")
        w_in = sem("w_in")
        idx_in = [sem(f"idx_in{c}") for c in range(CHUNKS)]
        bias_in = sem("bias_in")
        bias_laid = [sem(f"bias_laid{c}") for c in range(CHUNKS)]
        gathered = [sem(f"gathered{c}") for c in range(CHUNKS)]
        stored = [sem(f"stored{c}") for c in range(CHUNKS)]
        pool_const = sem("pool_const")
        prep_v = sem("prep_v")
        prep_a = sem("prep_a")
        abs_ps = sem("abs_ps")
        bias_ps = sem("bias_ps")
        st1_done = sem("st1_done")
        mv1_done = sem("mv1_done")
        rs1_sum = sem("rs1_sum")
        nm1_done = sem("nm1_done")
        rs1_done = sem("rs1_done")
        nb1_done = sem("nb1_done")
        xn_done = sem("xn_done")
        xt_ps = sem("xt_ps")
        xt_done = sem("xt_done")
        proj_ps = sem("proj_ps")
        xb_done = sem("xb_done")
        bt_done = sem("bt_done")
        xa_done = sem("xa_done")
        delta_done = sem("delta_done")
        carry_done = sem("carry_done")
        dsum_done = sem("dsum_done")
        dA_done = sem("dA_done")
        ct_done = sem("ct_done")
        lc_done = sem("lc_done")
        r0_done = sem("r0_done")
        ct2_done = sem("ct2_done")
        er_done = sem("er_done")
        rn_done = sem("rn_done")
        v_done = sem("v_done")
        z_done = sem("z_done")
        ssum_done = sem("ssum_done")
        g_done = sem("g_done")
        y_ps = sem("y_ps")
        h2_done = sem("h2_done")
        st2_done = sem("st2_done")
        mv2_done = sem("mv2_done")
        rs2_sum = sem("rs2_sum")
        rs2_done = sem("rs2_done")
        xn2_done = sem("xn2_done")
        end_added = sem("end_added")
        x2_ps = sem("x2_ps")
        x_hi_done = sem("x_hi_done")
        x_lo_done = sem("x_lo_done")
        hid_ps = sem("hid_ps")
        gelu_done = sem("gelu_done")
        sq_done = sem("sq_done")
        u_hi_done = sem("u_hi_done")
        u_done = sem("u_done")
        sq_sum = sem("sq_sum")
        o_ps = sem("o_ps")
        po_done = sem("po_done")
        sq_ps = sem("sq_ps")
        s_sq_done = sem("s_sq_done")
        tiny = sem("tiny")
        s_rs_done = sem("s_rs_done")
        fin_q = sem("fin_q")
        out_done = sem("out_done")

        held_v, held_p = sem("held_v"), sem("held_p")

        small = [(a_col, a_log), (bb_col, b_bias), (bd_col, d_bias), (g1_col, ln1_g), (b1n_col, ln1_b),
                 (b1_col, b1), (g2_col, ln2_g), (b2n_col, ln2_b), (wo2, wo_t)]
        rows = [(bo_b, bo), (b2_b, b2)]
        SMALL = 16 * (len(small) + len(rows) + 1)

        block = ctx.enter_context(nc.Block())

        @block.sync
        def _(sp):
            def load_idx(v):
                if not zero(v.pair):
                    sp.wait_ge(gathered[v.slot], v.pair * (16 * UT))
                sp.dma_start(idx[:, v.slot, :], tokens[bass.ds(v.pair * CHUNKS + v.slot, 1), :, :].rearrange(
                    "a p t -> (a p) t")).then_inc(idx_in[v.slot], 16)

            def store(v, g):
                sp.wait_ge(out_done, v.n * UT + (g + 1) * TILES)
                dst = out[bass.ds(v.pair * 2 + g, 1), v.slot * TG:(v.slot + 1) * TG, :].rearrange(
                    "a (t p) d -> p (a t) d", p=P)
                sp.dma_start(dst, E[:, v.slot, g * TILES:(g + 1) * TILES, :]).then_inc(stored[v.slot], 16)

            def lay_bias(v):
                if not zero(v.pair):
                    sp.wait_ge(stored[v.slot], v.pair * 32)
                sp.dma_start(E[:, v.slot, :, :], tok_bias_b[:, :].unsqueeze(1).broadcast_to([P, UT, D])).then_inc(
                    bias_laid[v.slot], 16)

            load_idx(Unit(0, 0))
            sp.dma_start(tok_bias_b[:, :], tok_bias.partition_broadcast(P)).then_inc(bias_in, 16)
            sp.wait_ge(bias_in, 16)
            lay_bias(Unit(0, 0))
            for c in range(1, CHUNKS - 1):
                load_idx(Unit(0, c))
            sp.dma_start(w1_f[:, :, :], w1_t.rearrange("(k p) n -> p k n", p=P)).then_inc(w_in, 16)
            sp.dma_start(w2_f[:, :, :], w2_t.rearrange("(k p) n -> p k n", p=P)).then_inc(w_in, 16)
            for dst, src in rows:
                sp.dma_start(dst[:, :], src.partition_broadcast(P)).then_inc(small_in, 16)
            for dst, src in small:
                sp.dma_start(dst[:, :], src).then_inc(small_in, 16)
            sp.dma_start(proj[:, :, :], proj_w.rearrange("(k p) n -> p k n", p=P)).then_inc(small_in, 16)

            for c in range(1, CHUNKS - 1):
                lay_bias(Unit(0, c))

            def stage(pair, k, left):
                if left >= 3:
                    load_idx(Unit(pair, k + 3))
                if k or not zero(pair):
                    store(Unit(pair, k - 1), 0)
                    store(Unit(pair, k - 1), 1)
                if left >= 3:
                    lay_bias(Unit(pair, k + 3))

            schedule(sp, stage)
            for g in range(2):
                store(Unit(PAIRS - 1, CHUNKS - 1), g)
            for c in range(CHUNKS):
                sp.wait_ge(stored[c], 32 * PAIRS)

        @block.gpsimd
        def _(pool):
            nc.gpsimd.memset(ones[:, :], 1.0).then_inc(pool_const, 1)
            nc.gpsimd.memset(ones_row[:, :], 1.0).then_inc(pool_const, 1)
            nc.gpsimd.memset(half[:, :], -0.5).then_inc(pool_const, 1)
            pool.wait_ge(pool_const, 3)
            nc.gpsimd.affine_select(out=ident[:, :], in_=ones[:, :], pattern=[[-1, P]], compare_op=ALU.is_equal,
                                    fill=0.0, base=0, channel_multiplier=1).then_inc(pool_const, 1)

            def gather(v):
                pool.wait_ge(idx_in[v.slot], (v.pair + 1) * 16)
                pool.wait_ge(bias_laid[v.slot], (v.pair + 1) * 16)
                pool.sem_inc(held_p, 1)
                for t in range(UT):
                    nc.gpsimd.indirect_dma_start(
                        out=E[:, v.slot, t, :], out_offset=None, in_=table,
                        in_offset=bass.IndirectOffsetOnAxis(ap=idx[:, v.slot, t:t + 1], axis=0),
                        compute_op=ALU.add,
                    ).then_inc(gathered[v.slot], 16)

            def add_row(v, row):
                return nc.gpsimd.tensor_tensor(E[:, v.slot, :, :], E[:, v.slot, :, :],
                                               row[:, :].unsqueeze(1).broadcast_to([P, UT, D]), ALU.add)

            def norm1(v):
                if not zero(v.n):
                    pool.wait_ge(xn_done, v.n * 2)
                pool.wait_ge(mv1_done, v.n + 1)
                pool.sem_inc(held_p, 1)
                nc.gpsimd.tensor_scalar(rs1[:, :], mv1[:, :, 1], 1.0, LN_EPS, ALU.mult, ALU.add).then_inc(rs1_sum, 1)
                pool.wait_ge(rs1_sum, v.n + 1)
                nc.gpsimd.tensor_tensor(rs1[:, :], rs1[:, :], half[:, :], ALU.pow).then_inc(rs1_done, 1)
                pool.wait_ge(nm1_done, v.n + 1)
                pool.wait_ge(rs1_done, v.n + 1)
                nc.gpsimd.tensor_tensor(nb1[:, :], nm1[:, :], rs1[:, :], ALU.mult).then_inc(nb1_done, 1)

            def norm2(v):
                pool.wait_ge(mv2_done, v.n + 1)
                pool.sem_inc(held_p, 1)
                nc.gpsimd.tensor_scalar(rs2[:, :], mv2[:, :, 1], 1.0 + LN_EPS, LN_EPS * LN_EPS, ALU.mult,
                                        ALU.add).then_inc(rs2_sum, 1)
                pool.wait_ge(rs2_sum, v.n + 1)
                nc.gpsimd.tensor_tensor(rs2[:, :], rs2[:, :], half[:, :], ALU.pow).then_inc(rs2_done, 1)

            def add_end(v):
                pool.wait_ge(xn2_done, v.n * 2 + 2)
                add_row(v, end_bias_b).then_inc(end_added, 1)

            def sum_squares(n):
                pool.wait_ge(sq_done, n * 4 + 4)
                nc.gpsimd.tensor_tensor(sq4[:, :, :], sq[:, 0:4, :], sq[:, 4:8, :], ALU.add).then_inc(sq_sum, 1)
                pool.wait_ge(sq_sum, n * 3 + 1)
                nc.gpsimd.tensor_tensor(sq4[:, 0:2, :], sq4[:, 0:2, :], sq4[:, 2:4, :], ALU.add).then_inc(sq_sum, 1)
                pool.wait_ge(sq_sum, n * 3 + 2)
                if not zero(n):
                    pool.wait_ge(sq_ps, n)
                nc.gpsimd.tensor_tensor(sq1[:, :], sq4[:, 0, :], sq4[:, 1, :], ALU.add).then_inc(sq_sum, 1)

            def root_hidden(n):
                pool.wait_ge(tiny, n * TINY + 5)
                nc.gpsimd.tensor_tensor(s_rs[:, :], s_var[:, :], half[:, 0:TILES], ALU.pow).then_inc(s_rs_done, 1)

            for c in range(3):
                gather(Unit(0, c))
            pool.wait_ge(pool_const, 4)
            pool.wait_ge(small_in, SMALL)
            norm1(Unit(0, 0))
            norm1(Unit(0, 1))
            norm2(Unit(0, 0))

            def stage(pair, k, left):
                n = Unit(pair, k).n
                if not zero(n):
                    root_hidden(n * 2 - 2)
                    sum_squares(n * 2 - 1)
                if left >= 2:
                    norm1(Unit(pair, k + 2))
                add_end(Unit(pair, k))
                if not zero(n):
                    root_hidden(n * 2 - 1)
                if left >= 1:
                    norm2(Unit(pair, k + 1))
                sum_squares(n * 2)
                if left >= 3:
                    gather(Unit(pair, k + 3))

            schedule(pool, stage)
            root_hidden(UNITS * 2 - 2)
            sum_squares(UNITS * 2 - 1)
            root_hidden(UNITS * 2 - 1)

        @block.scalar
        def _(act):
            def normalise1(v, h):
                act.wait_ge(nb1_done, v.n + 1)
                if not zero(v.n):
                    act.wait_ge(xt_ps, v.n * 2)
                for t in range(h * TILES, (h + 1) * TILES):
                    last = nc.scalar.activation(xn[:, t, :], E[:, v.slot, t, :], ACT.Identity, scale=rs1[:, t:t + 1],
                                                bias=nb1[:, t:t + 1])
                    if t % TILES == TILES - 1:
                        last.then_inc(xn_done, 1)

            def copy_xt(v, h):
                act.wait_ge(xt_ps, v.n * 2 + (h + 1))
                if not zero(v.n):
                    act.wait_ge(proj_ps, v.n)
                nc.scalar.copy(xnT[:, 0, h, :], T[0][:, :])
                nc.scalar.copy(xnT[:, 1, h, :], T[1][:, :]).then_inc(xt_done, 1)

            def projected(v):
                act.wait_ge(proj_ps, v.n + 1)
                if not zero(v.n):
                    act.wait_ge(delta_done, v.n)
                nc.scalar.activation(xb[0:N, :], X[0][N:P, :], ACT.Identity, bias=bd_col[N:P, :]).then_inc(xb_done, 1)
                nc.scalar.activation(xb[N:P, :], X[1][0:N, :], ACT.Identity, bias=bd_col[0:N, :]).then_inc(xb_done, 1)
                if not zero(v.n):
                    act.wait_ge(z_done, v.n)
                nc.scalar.activation(bt[0:N, :], X[0][0:N, :], ACT.Identity, bias=bb_col[0:N, :]).then_inc(bt_done, 1)
                nc.scalar.activation(bt[N:P, :], X[1][N:P, :], ACT.Identity, bias=bb_col[N:P, :]).then_inc(bt_done, 1)

            def softplus_part(v):
                act.wait_ge(xb_done, v.n * 2 + 2)
                nc.scalar.activation(xa[:, :], xb[:, :], ACT.Abs).then_inc(xa_done, 1)
                act.wait_ge(xa_done, v.n * 3 + 1)
                nc.scalar.activation(xa[:, :], xa[:, :], ACT.Exp, scale=-1.0).then_inc(xa_done, 1)
                act.wait_ge(xa_done, v.n * 3 + 2)
                nc.scalar.activation(xa[:, :], xa[:, :], ACT.Ln, bias=1.0).then_inc(xa_done, 1)

            def decay_part(v):
                act.wait_ge(delta_done, v.n + 1)
                if not zero(v.n):
                    act.wait_ge(v_done, v.n)
                nc.scalar.activation(dA[:, :], delta[:, :], ACT.Exp, scale=a_neg[:, :]).then_inc(dA_done, 1)
                act.wait_ge(dsum_done, v.n + 1)
                if not zero(v.n):
                    act.wait_ge(er_done, v.n)
                nc.scalar.activation(ct[:, :], dsum[:, v.slot % 2, 0:TG], ACT.Exp, scale=a_neg[:, :]).then_inc(ct_done, 1)
                act.wait_ge(ct_done, v.n + 1)
                nc.scalar.activation(lc[:, :], ct[:, :], ACT.Ln, bias=eps_col[:, :]).then_inc(lc_done, 1)
                act.wait_ge(lc_done, v.n + 1)
                if not zero(v.n):
                    act.wait_ge(rn_done, v.n)
                nc.scalar.activation(r0[:, :], lc[:, :], ACT.Exp, scale=-1.0).then_inc(r0_done, 1)
                if not zero(v.n):
                    act.wait_ge(g_done, v.n)
                nc.scalar.activation(ct2[:, :], ct[:, :], ACT.Square).then_inc(ct2_done, 1)

            def high_x(v, g):
                n = v.n * 2 + g
                act.wait_ge(x2_ps, n + 1)
                if not zero(v.n):
                    act.wait_ge(hid_ps, (n - 1) * KH)
                for k in range(KD):
                    nc.scalar.activation(x_hi[:, g, k, :], T[k][:, :], ACT.Identity,
                                         scale=g1_s[:, k:k + 1]).then_inc(x_hi_done, 1)

            def gelu(v, g, m):
                n = v.n * 2 + g
                act.wait_ge(hid_ps, n * KH + (m + 1))
                if not zero(n):
                    act.wait_ge(u_done, n * KH + (m + 1 - KH))
                    if m % 2 == 0:
                        act.wait_ge(sq_done, n * 4 + (m // 2 - 3))
                nc.scalar.activation(gf[:, m, :], H[m % 2][:, :], ACT.Gelu, scale=gelu_scale[:, :],
                                     bias=b1_eff[:, m:m + 1]).then_inc(gelu_done, 1)

            def square(v, g, m):
                n = v.n * 2 + g
                if m == 0 and not zero(n):
                    act.wait_ge(sq_sum, n * 3 - 2)
                act.wait_ge(gelu_done, n * KH + (m + 2))
                nc.scalar.activation(sq[:, m:m + 2, :], gf[:, m:m + 2, :], ACT.Square).then_inc(sq_done, 1)

            def copy_out(v, g, t):
                n = v.n * 2 + g
                act.wait_ge(o_ps, n * TILES + (t + 1))
                if t == 0 and not zero(v.n):
                    act.wait_ge(out_done, (n - 1) * TILES)
                nc.scalar.copy(po[:, g, t, :], O[t % 2][:, 0:WO]).then_inc(po_done, 1)

            def copy_squares(n):
                act.wait_ge(sq_ps, n + 1)
                if not zero(n):
                    act.wait_ge(tiny, n * TINY - (TINY - 4))
                nc.scalar.copy(s_sq[:, :], SQ_PS).then_inc(s_sq_done, 1)

            nc.scalar.preload_act_table_set("natural_log_exp_and_others")
            act.wait_ge(small_in, SMALL)
            nc.scalar.activation(a_soft[:, :], a_col[:, :], ACT.Abs).then_inc(prep_a, 1)
            act.wait_ge(prep_a, 1)
            nc.scalar.activation(a_soft[:, :], a_soft[:, :], ACT.Exp, scale=-1.0).then_inc(prep_a, 1)
            act.wait_ge(prep_a, 2)
            nc.scalar.activation(a_soft[:, :], a_soft[:, :], ACT.Ln, bias=1.0).then_inc(prep_a, 1)
            def embeddings_to_projections(v):
                return [lambda: normalise1(v, 0), lambda: normalise1(v, 1), lambda: copy_xt(v, 0),
                        lambda: copy_xt(v, 1), lambda: projected(v)]

            first, second = Unit(0, 0), Unit(0, 1)
            for f in embeddings_to_projections(first):
                f()
            softplus_part(first)
            decay_part(first)
            for f in embeddings_to_projections(second):
                f()
            high_x(first, 0)

            def stage(pair, k, left):
                u, after, then = Unit(pair, k), Unit(pair, k + 1), Unit(pair, k + 2)
                before, n = Unit(pair, k - 1), u.n * 2
                gelu(u, 0, 0)
                if not zero(u.n):
                    copy_out(before, 0, 3)
                gelu(u, 0, 1)
                high_x(u, 1)
                gelu(u, 0, 2)
                gelu(u, 0, 3)
                if left >= 1:
                    nc.scalar.preload_act_table_set("natural_log_exp_and_others")
                    softplus_part(after)
                if not zero(u.n):
                    copy_out(before, 1, 0)
                if left >= 1:
                    decay_part(after)
                if not zero(u.n):
                    copy_out(before, 1, 1)
                gelu(u, 0, 4)
                gelu(u, 0, 5)
                if not zero(u.n):
                    copy_out(before, 1, 2)
                if left >= 2:
                    normalise1(then, 0)
                if not zero(u.n):
                    copy_squares(n - 1)
                square(u, 0, 0)
                gelu(u, 0, 6)
                if left >= 2:
                    normalise1(then, 1)
                if not zero(u.n):
                    copy_out(before, 1, 3)
                square(u, 0, 2)
                gelu(u, 0, 7)
                square(u, 0, 4)
                if left >= 2:
                    copy_xt(then, 0)
                square(u, 0, 6)
                gelu(u, 1, 0)
                gelu(u, 1, 1)
                if left >= 2:
                    copy_xt(then, 1)
                copy_out(u, 0, 0)
                gelu(u, 1, 2)
                gelu(u, 1, 3)
                copy_out(u, 0, 1)
                if left >= 2:
                    projected(then)
                gelu(u, 1, 4)
                square(u, 1, 0)
                gelu(u, 1, 5)
                copy_out(u, 0, 2)
                square(u, 1, 2)
                gelu(u, 1, 6)
                square(u, 1, 4)
                if left >= 1:
                    high_x(after, 0)
                gelu(u, 1, 7)
                copy_squares(n)
                square(u, 1, 6)

            schedule(act, stage)
            copy_out(Unit(PAIRS - 1, CHUNKS - 1), 0, 3)
            for t in range(TILES):
                copy_out(Unit(PAIRS - 1, CHUNKS - 1), 1, t)
            copy_squares(UNITS * 2 - 1)

        @block.vector
        def _(dve):
            steps = [0]

            def link(ins):
                steps[0] += 1
                ins.then_inc(prep_v, 1)
                dve.wait_ge(prep_v, steps[0])

            dve.wait_ge(w_in, 32)
            link(nc.vector.memset(eps_col[:, :], EPS))
            link(nc.vector.tensor_reduce(absum[:, 0:1], w1_f[:, :, :], AX.XY, ALU.add, apply_absolute_value=True))
            link(nc.vector.tensor_reduce(absum[:, 1:2], w2_f[:, :, :], AX.XY, ALU.add, apply_absolute_value=True))
            assert steps[0] == ABSUM_STEPS
            dve.wait_ge(abs_ps, 1)
            link(nc.vector.tensor_scalar(wscale[:, :], X[0][:, 0:2], 1.0 / (D * HID), 1e-5, ALU.mult, ALU.max))
            link(nc.vector.reciprocal(winv[:, :], wscale[:, :]))
            link(nc.vector.tensor_scalar(gelu_scale[:, :], wscale[:, 0:1], 1.0 / XS, None, ALU.mult))
            link(nc.vector.tensor_scalar(alpha_scale[:, :], wscale[:, 1:2], 1.0 / US, None, ALU.mult))
            for i, (w, c) in enumerate(((w1_f, KD), (w2_f, KH))):
                flat = w.rearrange("p a b -> p (a b)")
                link(nc.vector.tensor_scalar(scratch, flat, winv[:, i:i + 1], 0.5, ALU.mult, ALU.is_gt))
                link(nc.vector.tensor_scalar(flat, flat, winv[:, i:i + 1], -0.5, ALU.mult, ALU.is_lt))
                link(nc.vector.tensor_tensor(flat, scratch, flat, ALU.subtract))
            link(nc.vector.tensor_copy(t1[:, :, :], w1_f[:, :, :]))
            dve.wait_ge(small_in, SMALL)
            link(nc.vector.tensor_scalar(g2_zero[:, :], g2_col[:, :], 0.0, None, ALU.is_equal))
            link(nc.vector.tensor_scalar(g2_some[:, :], g2_zero[:, :], -1.0, 1.0, ALU.mult, ALU.add))
            link(nc.vector.tensor_tensor(g2_safe[:, :], g2_col[:, :], g2_zero[:, :], ALU.add))
            link(nc.vector.tensor_scalar(g2_s[:, :], g2_safe[:, :], US, None, ALU.mult))
            link(nc.vector.reciprocal(g2_inv[:, :], g2_safe[:, :]))
            for k in range(KH):
                link(nc.vector.tensor_scalar(t2[:, k, 0:D], w2_f[:, k, :], g2_some[:, k:k + 1], None, ALU.mult))
            link(nc.vector.tensor_copy(t2[:, :, D], g2_inv[:, :]))
            link(nc.vector.tensor_tensor(t2[:, :, D + 1], g2_inv[:, :], t2[:, :, D], ALU.subtract))
            link(nc.vector.tensor_copy(wide, g2_col[:, :].unsqueeze(2).broadcast_to([P, KH, P])))
            link(nc.vector.tensor_copy(wide2, b2n_col[:, :].unsqueeze(2).broadcast_to([P, KH, P])))
            assert steps[0] == WIDE_STEPS
            link(nc.vector.tensor_scalar(g1_s[:, :], g1_col[:, :], XS, None, ALU.mult))
            dve.wait_ge(prep_a, 3)
            link(nc.vector.scalar_tensor_tensor(a_neg[:, :], a_col[:, :], 0.0, a_soft[:, :], ALU.max, ALU.add))
            link(nc.vector.tensor_scalar(a_neg[:, :], a_neg[:, :], -1.0, None, ALU.mult))
            link(nc.vector.tensor_scalar(a_inv[:, :], a_neg[:, :], EPS, -1.0, ALU.add, ALU.mult))
            link(nc.vector.reciprocal(a_inv[:, :], a_inv[:, :]))
            dve.wait_ge(bias_ps, 1)
            link(nc.vector.scalar_tensor_tensor(b1_eff[:, :], T[0][:, 0:KH], wscale[:, 0:1], b1_col[:, :], ALU.mult,
                                                ALU.add))
            link(nc.vector.tensor_copy(colsum_b[:, :], X[0][:, 0:D]))
            link(nc.vector.scalar_tensor_tensor(end_bias_b[:, :], X[1][:, 0:D], wscale[:, 1:2], b2_b[:, :], ALU.mult,
                                                ALU.add))
            link(nc.vector.memset(ones_bf[:, :], 1.0))
            link(nc.vector.memset(bo_parts[:, :, :], 0.0))
            for q in (0, 32, 64):
                row = bo_parts[q:q + 1, 0, :]
                link(nc.vector.tensor_copy(row, bo_b[q:q + 1, :] if q == 0 else bo_rest[q:q + 1, :]))
                link(nc.vector.tensor_copy(bo_parts[q:q + 1, 1, :], row))
                if q == 0:
                    link(nc.vector.tensor_copy(bo_hi[:, :], bo_b[:, :]))
                    link(nc.vector.tensor_tensor(bo_rest[:, :], bo_b[:, :], bo_hi[:, :], ALU.subtract))
                if q == 32:
                    link(nc.vector.tensor_copy(bo_hi[:, :], bo_rest[:, :]))
                    link(nc.vector.tensor_tensor(bo_rest[:, :], bo_rest[:, :], bo_hi[:, :], ALU.subtract))
            assert steps[0] == PREP_STEPS
            dve.wait_ge(pool_const, 4)

            def stats(v, st, mv, st_done, mv_done):
                for t in range(UT):
                    last = nc.vector.bn_stats(st[:, t, :], E[:, v.slot, t, :])
                last.then_inc(st_done, 1)
                dve.wait_ge(st_done, v.n + 1)
                dve.sem_inc(held_v, 1)
                for t in range(UT):
                    last = nc.vector.bn_aggr(mv[:, t, :], st[:, t, :])
                last.then_inc(mv_done, 1)

            def normalise(v, dst, mv, rs, done):
                for t in range(UT):
                    last = nc.vector.tensor_scalar(dst[:, t, :], E[:, v.slot, t, :], mv[:, t, 0:1], rs[:, t:t + 1],
                                                   ALU.subtract, ALU.mult)
                    if t % TILES == TILES - 1:
                        last.then_inc(done, 1)

            def stats1(v):
                dve.wait_ge(gathered[v.slot], (v.pair + 1) * (16 * UT))
                if not zero(v.n):
                    dve.wait_ge(nb1_done, v.n)
                stats(v, st1, mv1, st1_done, mv1_done)
                dve.wait_ge(mv1_done, v.n + 1)
                nc.vector.tensor_scalar(nm1[:, :], mv1[:, :, 0], -1.0, None, ALU.mult).then_inc(nm1_done, 1)

            def step_sums(v):
                b = v.slot % 2
                dve.wait_ge(xa_done, v.n * 3 + 3)
                if not zero(v.n):
                    dve.wait_ge(dA_done, v.n)
                nc.vector.scalar_tensor_tensor(delta[:, :], xb[:, :], 0.0, xa[:, :], ALU.max, ALU.add).then_inc(delta_done, 1)
                if not zero(v.n):
                    dve.wait_ge(ct_done, v.n)
                if v.slot == 0:
                    nc.vector.memset(dsum[:, b, 0:1], 0.0).then_inc(carry_done, 1)
                else:
                    dve.wait_ge(dsum_done, v.n)
                    nc.vector.tensor_copy(dsum[:, b, 0:1], dsum[:, 1 - b, TG:TG + 1]).then_inc(carry_done, 1)
                dve.wait_ge(delta_done, v.n + 1)
                dve.wait_ge(carry_done, v.n + 1)
                nc.vector.tensor_tensor_scan(dsum[:, b, 1:TG + 1], ones_row[:, :], delta[:, :], dsum[:, b, 0:1],
                                             ALU.mult, ALU.add).then_inc(dsum_done, 1)

            def recurrence(v):
                b = v.slot % 2
                dve.wait_ge(r0_done, v.n + 1)
                nc.vector.scalar_tensor_tensor(er[:, :], ct[:, :], EPS, r0[:, :], ALU.add, ALU.mult).then_inc(er_done, 1)
                dve.wait_ge(er_done, v.n + 1)
                nc.vector.scalar_tensor_tensor(rn[:, :], er[:, :], -2.0, r0[:, :], ALU.add, ALU.mult).then_inc(rn_done, 1)
                dve.wait_ge(rn_done, v.n + 1)
                dve.wait_ge(dA_done, v.n + 1)
                nc.vector.scalar_tensor_tensor(zz[:, :], dA[:, :], -1.0, rn[:, :], ALU.add, ALU.mult).then_inc(v_done, 1)
                dve.wait_ge(v_done, v.n + 1)
                dve.wait_ge(bt_done, v.n * 2 + 2)
                nc.vector.tensor_tensor(zz[:, :], bt[:, :], zz[:, :], ALU.mult).then_inc(z_done, 1)
                dve.wait_ge(z_done, v.n + 1)
                if v.slot:
                    dve.wait_ge(ssum_done, v.n)
                nc.vector.tensor_tensor_scan(ssum[:, b, :], ones_row[:, :], zz[:, :],
                                             ssum[:, 1 - b, TG - 1:TG] if v.slot else 0.0,
                                             ALU.mult, ALU.add).then_inc(ssum_done, 1)
                dve.wait_ge(ssum_done, v.n + 1)
                dve.wait_ge(ct2_done, v.n + 1)
                if not zero(v.n):
                    dve.wait_ge(y_ps, v.n * 4)
                nc.vector.scalar_tensor_tensor(G[:, :], ssum[:, b, :], a_inv[:, :], ct2[:, :], ALU.mult,
                                               ALU.mult).then_inc(g_done, 1)

            def residual(v, q):
                dve.wait_ge(y_ps, v.n * 4 + (q + 1))
                e = E[:, v.slot, 2 * q:2 * q + 2, :].rearrange("p t d -> p (t d)")
                nc.vector.tensor_tensor(e, X[q % 2][:, :], e, ALU.add).then_inc(h2_done, 1)

            def stats2(v):
                dve.wait_ge(h2_done, v.n * 4 + 4)
                stats(v, st2, mv2, st2_done, mv2_done)

            def normalise2(v):
                dve.wait_ge(rs2_done, v.n + 1)
                if not zero(v.n):
                    dve.wait_ge(x2_ps, v.n * 2)
                normalise(v, xn2, mv2, rs2, xn2_done)

            def low_x(v, g):
                n = v.n * 2 + g
                if not zero(v.n):
                    dve.wait_ge(hid_ps, (n - 1) * KH)
                for k in range(KD):
                    dve.wait_ge(x_hi_done, n * 2 + (k + 1))
                    nc.vector.scalar_tensor_tensor(x_lo[:, g, k, :], T[k][:, :], g1_s[:, k:k + 1], x_hi[:, g, k, :],
                                                   ALU.mult, ALU.subtract).then_inc(x_lo_done, 1)

            def step(n, i, ins):
                ins.then_inc(tiny, 1)
                dve.wait_ge(tiny, n * TINY + i)

            def hidden_variance(n, g):
                dve.wait_ge(po_done, n * TILES + TILES)
                step(n, 1, nc.vector.tensor_tensor(s_sum[:, :], po[:, g, :, D], po[:, g, :, D + 1], ALU.add))
                step(n, 2, nc.vector.tensor_scalar(s_mean[:, :], s_sum[:, :], 1.0 / (US * HID), None, ALU.mult))
                step(n, 3, nc.vector.tensor_tensor(s_msq[:, :], s_mean[:, :], s_mean[:, :], ALU.mult))
                dve.wait_ge(s_sq_done, n + 1)
                step(n, 4, nc.vector.scalar_tensor_tensor(s_var[:, :], s_sq[:, :], 1.0 / HID, s_msq[:, :], ALU.mult,
                                                          ALU.subtract))
                step(n, 5, nc.vector.tensor_scalar(s_var[:, :], s_var[:, :], 0.0, LN_EPS, ALU.max, ALU.add))

            def hidden_scales(n):
                dve.wait_ge(s_rs_done, n + 1)
                step(n, 6, nc.vector.tensor_scalar(s_alpha[:, :], s_rs[:, :], alpha_scale[:, :], None, ALU.mult))
                step(n, 7, nc.vector.scalar_tensor_tensor(s_beta[:, :], s_mean[:, :], -US, s_alpha[:, :], ALU.mult,
                                                          ALU.mult))

            def finish_first(v, g, t):
                n = v.n * 2 + g
                if t == 0:
                    dve.wait_ge(tiny, n * TINY + 7)
                    dve.wait_ge(end_added, v.n + 1)
                nc.vector.scalar_tensor_tensor(E[:, v.slot, g * TILES + t, :], colsum_b[:, :], s_beta[:, t:t + 1],
                                               E[:, v.slot, g * TILES + t, :], ALU.mult, ALU.add).then_inc(fin_q, 1)

            def finish_last(v, g, t):
                n = v.n * 2 + g
                dve.wait_ge(fin_q, n * TILES + (t + 1))
                nc.vector.scalar_tensor_tensor(E[:, v.slot, g * TILES + t, :], po[:, g, t, 0:D], s_alpha[:, t:t + 1],
                                               E[:, v.slot, g * TILES + t, :], ALU.mult, ALU.add).then_inc(out_done, 1)

            def finish(v, g):
                for t in range(TILES):
                    finish_first(v, g, t)
                for t in range(TILES):
                    finish_last(v, g, t)

            def split_hidden(v, g, chunks):
                n = v.n * 2 + g
                if chunks[0] == 0 and not zero(v.n):
                    dve.wait_ge(o_ps, (n - 1) * TILES)

                def high(m):
                    dve.wait_ge(gelu_done, n * KH + (m + 1))
                    nc.vector.tensor_scalar(u_hi[:, g, m, :], gf[:, m, :], g2_s[:, m:m + 1], None,
                                            ALU.mult).then_inc(u_hi_done, 1)

                high(chunks[0])
                for m in chunks:
                    if m + 1 in chunks:
                        high(m + 1)
                    dve.wait_ge(u_hi_done, n * KH + (m + 1))
                    nc.vector.scalar_tensor_tensor(u_lo[:, g, m, :], gf[:, m, :], g2_s[:, m:m + 1], u_hi[:, g, m, :],
                                                   ALU.mult, ALU.subtract).then_inc(u_done, 1)

            first = Unit(0, 0)
            stats1(first)
            step_sums(first)
            recurrence(first)
            stats1(Unit(0, 1))
            for q in range(4):
                residual(first, q)
            stats2(first)
            normalise2(first)
            low_x(first, 0)

            def stage(pair, k, left):
                u, after, then = Unit(pair, k), Unit(pair, k + 1), Unit(pair, k + 2)
                before, n = Unit(pair, k - 1), u.n * 2
                split_hidden(u, 0, (0, 1))
                if not zero(u.n):
                    hidden_variance(n - 2, 0)
                low_x(u, 1)
                split_hidden(u, 0, (2, 3))
                if left >= 1:
                    step_sums(after)
                if left >= 2:
                    stats1(then)
                if not zero(u.n):
                    hidden_scales(n - 2)
                if left >= 1:
                    recurrence(after)
                if not zero(u.n):
                    for t in range(TILES):
                        finish_first(before, 0, t)
                if left >= 1:
                    residual(after, 0)
                    residual(after, 1)
                if not zero(u.n):
                    for t in range(TILES):
                        finish_last(before, 0, t)
                split_hidden(u, 0, (4, 5))
                if left >= 1:
                    residual(after, 2)
                    residual(after, 3)
                split_hidden(u, 0, (6, 7))
                if not zero(u.n):
                    hidden_variance(n - 1, 1)
                if left >= 1:
                    stats2(after)
                if not zero(u.n):
                    hidden_scales(n - 1)
                    finish(before, 1)
                if left >= 1:
                    normalise2(after)
                split_hidden(u, 1, range(KH - 1))
                if left >= 1:
                    low_x(after, 0)
                split_hidden(u, 1, (KH - 1,))

            schedule(dve, stage)
            last, n = Unit(PAIRS - 1, CHUNKS - 1), UNITS * 2 - 1
            hidden_variance(n - 1, 0)
            hidden_scales(n - 1)
            finish(last, 0)
            hidden_variance(n, 1)
            hidden_scales(n)
            finish(last, 1)

        @block.tensor
        def _(pe):
            pe.wait_ge(pool_const, 4)
            pe.wait_ge(prep_v, ABSUM_STEPS)
            nc.tensor.matmul(X[0][:, 0:2], ones[:, :], absum[:, :], start=True, stop=True).then_inc(abs_ps, 1)
            pe.wait_ge(prep_v, WIDE_STEPS)
            for m in range(KH):
                for k in range(KD):
                    nc.tensor.matmul(T[0][:, m:m + 1], w1_f[:, k, m * P:(m + 1) * P], b1n_col[:, k:k + 1],
                                     start=(k == 0), stop=(k == KD - 1))
            for w, x in ((wide, X[0]), (wide2, X[1])):
                for k in range(KH):
                    last = nc.tensor.matmul(x[:, 0:D], w[:, k, :], w2_f[:, k, :], start=(k == 0), stop=(k == KH - 1))
            last.then_inc(bias_ps, 1)
            pe.wait_ge(prep_v, PREP_STEPS)

            def turn(x, g, done):
                for k in range(KD):
                    for t in range(TILES):
                        last = nc.tensor.transpose(T[k][:, t * P:(t + 1) * P], x[:, g * TILES + t, k * P:(k + 1) * P],
                                                   ident[:, :])
                last.then_inc(done, 1)

            def turn_embeddings(v, h):
                pe.wait_ge(xn_done, v.n * 2 + (h + 1))
                turn(xn, h, xt_ps)

            def project(v):
                pe.wait_ge(xt_done, v.n * 2 + 2)
                if not zero(v.n):
                    pe.wait_ge(h2_done, v.n * 4)
                for h in range(2):
                    for k in range(KD):
                        last = nc.tensor.matmul(X[h][:, :], proj[:, k, h * P:(h + 1) * P], xnT[:, k, h, :],
                                                start=(k == 0), stop=(k == KD - 1))
                last.then_inc(proj_ps, 1)

            def attention_out(v, q):
                h = q // 2
                pe.wait_ge(g_done, v.n + 1)
                pe.wait_ge(bt_done, v.n * 2 + 2)
                if q >= 2 or not zero(v.n):
                    pe.wait_ge(h2_done, v.n * 4 + (q - 1 if q >= 2 else 0))
                nc.tensor.matmul(X[q % 2][:, :], ones_bf[:, :], bo_parts[:, :, :], start=True, stop=False)
                for i in range(2):
                    t = (q % 2) * 2 + i
                    last = nc.tensor.matmul(X[q % 2][:, i * D:(i + 1) * D], G[h * N:(h + 1) * N, t * P:(t + 1) * P],
                                            wo2[h * N:(h + 1) * N, :], start=False, stop=(i == 1))
                last.then_inc(y_ps, 1)

            def turn_stream(v, g):
                pe.wait_ge(xn2_done, v.n * 2 + (g + 1))
                turn(xn2, g, x2_ps)

            def square_sums(n):
                pe.wait_ge(sq_sum, n * 3 + 3)
                pe.wait_ge(po_done, n * TILES + 3)
                for t in range(TILES):
                    last = nc.tensor.matmul(SQ_PS[:, t:t + 1], sq1[:, t * P:(t + 1) * P], ones[:, 0:1], start=True,
                                            stop=True)
                last.then_inc(sq_ps, 1)

            def first_product(v, g, chunks):
                n = v.n * 2 + g
                if chunks[0] == 0:
                    pe.wait_ge(x_hi_done, n * 2 + 2)
                    pe.wait_ge(x_lo_done, n * 2 + 2)
                for m in chunks:
                    if not (zero(n) and m < 2):
                        pe.wait_ge(gelu_done, n * KH + (m - 1))
                    for k in range(KD):
                        for x in (x_hi, x_lo):
                            last = nc.tensor.matmul(H[m % 2][:, :], t1[:, k, m * P:(m + 1) * P], x[:, g, k, :],
                                                    start=(k == 0 and x is x_hi), stop=(k == KD - 1 and x is x_lo))
                    last.then_inc(hid_ps, 1)

            def second_product(v, g, t, chunks=range(KH)):
                n = v.n * 2 + g
                if chunks[0] == 0:
                    if t == 0 and not zero(n):
                        pe.wait_ge(s_sq_done, n)
                    if not (zero(n) and t < 2):
                        pe.wait_ge(po_done, n * TILES + (t - 1))
                for k in chunks:
                    if t == 0:
                        pe.wait_ge(u_done, n * KH + (k + 1))
                    for x in (u_hi, u_lo):
                        last = nc.tensor.matmul(O[t % 2][:, 0:WO], x[:, g, k, t * P:(t + 1) * P], t2[:, k, :],
                                                start=(k == 0 and x is u_hi), stop=(k == KH - 1 and x is u_lo))
                if k == KH - 1:
                    last.then_inc(o_ps, 1)

            def banks_read(xt=None, x=None):
                if xt is not None:
                    pe.wait_ge(xt_done, xt)
                else:
                    pe.wait_ge(x_hi_done, x * 2)
                    pe.wait_ge(x_lo_done, x * 2)

            first, second = Unit(0, 0), Unit(0, 1)
            turn_embeddings(first, 0)
            banks_read(xt=1)
            turn_embeddings(first, 1)
            project(first)
            for q in range(4):
                attention_out(first, q)
            turn_embeddings(second, 0)
            banks_read(xt=3)
            turn_embeddings(second, 1)
            project(second)
            turn_stream(first, 0)

            def stage(pair, k, left):
                u, after, then, before = Unit(pair, k), Unit(pair, k + 1), Unit(pair, k + 2), Unit(pair, k - 1)
                n = u.n * 2
                first_product(u, 0, (0, 1))
                banks_read(x=n + 1)
                turn_stream(u, 1)
                first_product(u, 0, (2, 3, 4, 5))
                if not zero(u.n):
                    for t in range(TILES):
                        second_product(before, 1, t)
                first_product(u, 0, (6,))
                if not zero(u.n):
                    square_sums(n - 1)
                first_product(u, 0, (7,))
                second_product(u, 0, 0, range(KH // 2))
                if left >= 1:
                    for q in range(4):
                        attention_out(after, q)
                if left >= 2:
                    banks_read(x=n + 2)
                    turn_embeddings(then, 0)
                for m in range(KH):
                    first_product(u, 1, (m,))
                    if m == 0 and left >= 2:
                        banks_read(xt=then.n * 2 + 1)
                        turn_embeddings(then, 1)
                    if m == 2 and left >= 2:
                        project(then)
                    if m == 5 and left >= 1:
                        if left >= 2:
                            banks_read(xt=then.n * 2 + 2)
                        else:
                            banks_read(x=n + 2)
                        turn_stream(after, 0)
                    if m:
                        second_product(u, 0, m // 2, (range(KH // 2), range(KH // 2, KH))[m % 2])
                    if m == 6:
                        square_sums(n)

            schedule(pe, stage)
            last_unit = Unit(PAIRS - 1, CHUNKS - 1)
            for t in range(TILES):
                second_product(last_unit, 1, t)
            square_sums(UNITS * 2 - 1)


ABSUM_STEPS = 3
WIDE_STEPS = 3 + 4 + 6 + 1 + 5 + KH + 4
PREP_STEPS = WIDE_STEPS + 1 + 4 + 3 + 12


def kernel(x, L0_tok_weight, L0_tok_bias, L0_attn_A_log, L0_attn_WB, L0_attn_bB, L0_attn_WC, L0_attn_bC, L0_attn_Wd,
           L0_attn_bd, L0_attn_Wo, L0_attn_bo, L0_ffn_ln1_g, L0_ffn_ln1_b, L0_ffn_w1, L0_ffn_b1, L0_ffn_ln2_g,
           L0_ffn_ln2_b, L0_ffn_w2, L0_ffn_b2):
    import numpy as np
    import concourse.bacc as bacc
    from concourse.bass_utils import run_bass_kernel_spmd

    def twice(a):
        return np.concatenate([a, a]).reshape(P, 1)

    def column(a):
        return np.ascontiguousarray(np.asarray(a).reshape(-1, P).T)

    wb, wd = np.asarray(L0_attn_WB).T, np.repeat(np.asarray(L0_attn_Wd).T, N, axis=1)
    wo = np.asarray(L0_attn_Wo).T
    arrays = {
        "tokens": np.ascontiguousarray(np.asarray(x).reshape(PAIRS, 2, CHUNKS, TILES, P).transpose(0, 2, 4, 1, 3)
                                       .reshape(UNITS, P, UT)),
        "table": np.ascontiguousarray(np.asarray(L0_tok_weight).T),
        "tok_bias": np.asarray(L0_tok_bias),
        "a_log": twice(np.asarray(L0_attn_A_log)),
        "b_bias": twice(np.asarray(L0_attn_bB)),
        "d_bias": np.repeat(np.asarray(L0_attn_bd), P).reshape(P, 1),
        "proj_w": np.ascontiguousarray(np.concatenate([wb, wd, wd, wb], axis=1)),
        "wo_t": np.ascontiguousarray(np.concatenate([wo, wo])),
        "bo": np.asarray(L0_attn_bo),
        "ln1_g": column(L0_ffn_ln1_g),
        "ln1_b": column(L0_ffn_ln1_b),
        "w1_t": np.ascontiguousarray(np.asarray(L0_ffn_w1).T),
        "b1": column(L0_ffn_b1),
        "ln2_g": column(L0_ffn_ln2_g),
        "ln2_b": column(L0_ffn_ln2_b),
        "w2_t": np.ascontiguousarray(np.asarray(L0_ffn_w2).T),
        "b2": np.asarray(L0_ffn_b2),
    }
    nc = bacc.Bacc("TRN2", target_bir_lowering=False, num_devices=1)
    given = {k: nc.dram_tensor(k, a.shape, mybir.dt.from_np(a.dtype), kind="ExternalInput").ap()
             for k, a in arrays.items()}
    out = nc.dram_tensor("out", (BATCH, SEQ, D), F32, kind="ExternalOutput").ap()
    lm_tower(nc, out=out, **given)
    return run_bass_kernel_spmd(nc, [arrays], core_ids=[0]).results[0]["out"]
```
